# Optimizing a Trainium2 kernel written in Bass

```python
import numpy as np
import jax
import jax.numpy as jnp

def _softmax(x, axis=-1):
    return jax.nn.softmax(x, axis=axis)
def _gelu(x):
    return jax.nn.gelu(x, approximate=True)
def _silu(x):
    return jax.nn.silu(x)
def _sigmoid(x):
    return jax.nn.sigmoid(x)
def _layernorm(x, axis=-1, eps=1e-5):
    m = jnp.mean(x, axis=axis, keepdims=True)
    v = jnp.var(x, axis=axis, keepdims=True)
    return (x - m) / jnp.sqrt(v + eps)
def _scatter_add(tgt, idx, src, axis=0):
    return tgt.at[idx].add(src)
def _segment_sum(src, seg, n):
    return jax.ops.segment_sum(src, seg, n)

kernel_name = 'mk_adj_preln_d4_adj_512_3dc6dd'

def setup_inputs(seed: int = 0):
    np.random.seed(seed)
    _w = jnp.asarray
    def _rec_inputs():
        import jax
        import jax.numpy as jnp
        _gk = jax.random.key(seed)
        x = -0.0002928 + 1 * jax.random.normal(jax.random.fold_in(_gk, 1), (128, 128, 512), jnp.float32)
        _a = jax.random.bernoulli(jax.random.fold_in(_gk, 2), 0.0625, (128, 128, 128))
        _a = jnp.logical_or(_a, jnp.swapaxes(_a, -1, -2))
        _a = jnp.logical_or(_a, jnp.eye(128, dtype=bool))
        adj = _a.astype(jnp.int32)
        return x, adj
    x, adj = _rec_inputs()
    def _L0_gnn_setup():
        import jax, jax.numpy as jnp
        import numpy as np
        ALPHA = 0.2

        def _leaky(x):
            return jnp.where(x >= 0, x, ALPHA * x)
        key = jax.random.key(seed)
        k1, k2, k3, k4 = jax.random.split(key, 4)
        B, N, F_in, F_out = (4, 2048, 512, 512)
        h = jax.random.normal(k1, (B, N, F_in), dtype=jnp.float32)
        W = jax.random.normal(k2, (F_in, F_out), dtype=jnp.float32) * 0.05
        a = jax.random.normal(k3, (2 * F_out, 1), dtype=jnp.float32) * 0.05
        adj = jax.random.randint(k4, (B, N, N), 0, 2, dtype=jnp.int32)
        return {'h': h, 'W': W, 'a': a, 'adj': adj}
    _L0_gnn_all = _L0_gnn_setup()
    _L0_gnn_in = {k: v for k, v in _L0_gnn_all.items() if k in ('W', 'a', )}
    del _L0_gnn_all

    def _L1_gnn_setup():
        import jax, jax.numpy as jnp
        import numpy as np
        ALPHA = 0.2
        MASK_VAL = -1000000000.0
        key = jax.random.key(seed)
        k1, k2, k3, k4 = jax.random.split(key, 4)
        B, N, F_in, F_out = (8, 2048, 512, 512)
        h = jax.random.normal(k1, (B, N, F_in), dtype=jnp.float32)
        adj = jax.random.randint(k2, (B, N, N), 0, 2, dtype=jnp.int32)

        def xavier(k, shape, gain=1.414):
            fan_in, fan_out = (shape[0], shape[1])
            bound = gain * np.sqrt(6.0 / (fan_in + fan_out))
            return jax.random.uniform(k, shape, jnp.float32, -bound, bound)
        W = xavier(k3, (F_in, F_out))
        a = xavier(k4, (2 * F_out, 1))
        return {'h': h, 'adj': adj, 'W': W, 'a': a}
    _L1_gnn_all = _L1_gnn_setup()
    _L1_gnn_in = {k: v for k, v in _L1_gnn_all.items() if k in ('W', 'a', )}
    del _L1_gnn_all

    def _L2_gnn_setup():
        import jax, jax.numpy as jnp
        import numpy as np
        ALPHA = 0.2
        NEG_INF = -1000000000.0
        key = jax.random.key(seed)
        k1, k2, k3, k4 = jax.random.split(key, 4)
        B, N, IN, OUT = (8, 2048, 512, 32)
        graph_input = jax.random.normal(k1, (B, N, IN), dtype=jnp.float32)
        adj = jax.random.randint(k2, (B, N, N), 0, 2, dtype=jnp.int32)
        W_fc = jax.random.normal(k3, (OUT, IN), dtype=jnp.float32) * (1.0 / np.sqrt(IN))
        W_attn = jax.random.normal(k4, (1, 2 * OUT), dtype=jnp.float32) * (1.0 / np.sqrt(2 * OUT))
        return {'graph_input': graph_input, 'adj': adj, 'W_fc': W_fc, 'W_attn': W_attn}
    _L2_gnn_all = _L2_gnn_setup()
    _L2_gnn_in = {k: v for k, v in _L2_gnn_all.items() if k in ('W_fc', 'W_attn', )}
    del _L2_gnn_all

    def _L3_gnn_setup():
        import jax, jax.numpy as jnp
        import numpy as np
        NEG_INF = -1000000000.0
        NEG_SLOPE = 0.2

        def gat_layer(x, mask, W, a_src, a_dst, bias, concat):
            B, N, _ = x.shape
            H, F = a_src.shape
            xl = (x @ W).reshape(B, N, H, F)
            asrc = jnp.einsum('bnhf,hf->bnh', xl, a_src)
            adst = jnp.einsum('bnhf,hf->bnh', xl, a_dst)
            e = jax.nn.leaky_relu(asrc[:, :, None, :] + adst[:, None, :, :], NEG_SLOPE)
            e = jnp.where(mask[..., None], e, NEG_INF)
            attn = jax.nn.softmax(e, axis=1)
            out = jnp.einsum('bsdh,bshf->bdhf', attn, xl)
            if concat:
                out = out.reshape(B, N, H * F)
            else:
                out = out.mean(axis=2)
            return out + bias
        key = jax.random.key(seed)
        ks = jax.random.split(key, 10)
        B, N, Din, Fh, H, Dout = (8, 1024, 512, 256, 4, 512)
        s = 0.05
        return {'adj': jax.random.randint(ks[0], (B, N, N), 0, 2, dtype=jnp.int32), 'x': jax.random.normal(ks[1], (B, N, Din), dtype=jnp.float32), 'W1': jax.random.normal(ks[2], (Din, H * Fh), dtype=jnp.float32) * s, 'att_src1': jax.random.normal(ks[3], (H, Fh), dtype=jnp.float32) * s, 'att_dst1': jax.random.normal(ks[4], (H, Fh), dtype=jnp.float32) * s, 'b1': jax.random.normal(ks[5], (H * Fh,), dtype=jnp.float32) * s, 'W2': jax.random.normal(ks[6], (H * Fh, Dout), dtype=jnp.float32) * s, 'att_src2': jax.random.normal(ks[7], (1, Dout), dtype=jnp.float32) * s, 'att_dst2': jax.random.normal(ks[8], (1, Dout), dtype=jnp.float32) * s, 'b2': jax.random.normal(ks[9], (Dout,), dtype=jnp.float32) * s}
    _L3_gnn_all = _L3_gnn_setup()
    _L3_gnn_in = {k: v for k, v in _L3_gnn_all.items() if k in ('W1', 'att_src1', 'att_dst1', 'b1', 'W2', 'att_src2', 'att_dst2', 'b2', )}
    del _L3_gnn_all

    return {
        "x": x,
        "adj": adj,
        "L0_gnn_W": _L0_gnn_in["W"],
        "L0_gnn_a": _L0_gnn_in["a"],
        "L1_gnn_W": _L1_gnn_in["W"],
        "L1_gnn_a": _L1_gnn_in["a"],
        "L2_gnn_W_fc": _L2_gnn_in["W_fc"],
        "L2_gnn_W_attn": _L2_gnn_in["W_attn"],
        "L3_gnn_W1": _L3_gnn_in["W1"],
        "L3_gnn_att_src1": _L3_gnn_in["att_src1"],
        "L3_gnn_att_dst1": _L3_gnn_in["att_dst1"],
        "L3_gnn_b1": _L3_gnn_in["b1"],
        "L3_gnn_W2": _L3_gnn_in["W2"],
        "L3_gnn_att_src2": _L3_gnn_in["att_src2"],
        "L3_gnn_att_dst2": _L3_gnn_in["att_dst2"],
        "L3_gnn_b2": _L3_gnn_in["b2"],
    }

def reference(x, adj, L0_gnn_W, L0_gnn_a, L1_gnn_W, L1_gnn_a, L2_gnn_W_fc, L2_gnn_W_attn, L3_gnn_W1, L3_gnn_att_src1, L3_gnn_att_dst1, L3_gnn_b1, L3_gnn_W2, L3_gnn_att_src2, L3_gnn_att_dst2, L3_gnn_b2):
    import jax
    import jax.numpy as jnp
    def _L0_gnn_ref(h, W, a, adj):
        import jax, jax.numpy as jnp
        import numpy as np
        ALPHA = 0.2

        def _leaky(x):
            return jnp.where(x >= 0, x, ALPHA * x)
        F_out = W.shape[1]
        Wh = jnp.matmul(h, W)
        Wh_sg = jax.lax.stop_gradient(Wh)
        a1 = a[:F_out, 0]
        a2 = a[F_out:, 0]
        s_i = Wh_sg @ a1
        s_j = Wh_sg @ a2
        e = _leaky(s_i[:, :, None] + s_j[:, None, :])
        e = jnp.where(adj > 0, e, jnp.float32(-9000000000000000.0))
        attention = jax.nn.softmax(e, axis=1)
        h_prime = jnp.einsum('bij,bjf->bif', attention, Wh)
        return _leaky(h_prime)

    def _L1_gnn_ref(h, adj, W, a):
        import jax, jax.numpy as jnp
        import numpy as np
        ALPHA = 0.2
        MASK_VAL = -1000000000.0
        Fout = W.shape[1]
        Wh = jnp.matmul(h, W)
        a1 = a[:Fout, 0]
        a2 = a[Fout:, 0]
        e_i = jnp.einsum('bnf,f->bn', Wh, a1)
        e_j = jnp.einsum('bnf,f->bn', Wh, a2)
        e = e_i[:, :, None] + e_j[:, None, :]
        e = jax.nn.leaky_relu(e, negative_slope=ALPHA)
        e = jnp.where(adj == 0, MASK_VAL, e)
        attention = jax.nn.softmax(e, axis=2)
        h_prime = jnp.matmul(attention, Wh)
        return jax.nn.elu(h_prime)

    def _L2_gnn_ref(graph_input, adj, W_fc, W_attn):
        import jax, jax.numpy as jnp
        import numpy as np
        ALPHA = 0.2
        NEG_INF = -1000000000.0
        h = jnp.einsum('bni,oi->bno', graph_input, W_fc)
        out_dim = W_fc.shape[0]
        a1 = W_attn[0, :out_dim]
        a2 = W_attn[0, out_dim:]
        f1 = jnp.einsum('bno,o->bn', h, a1)
        f2 = jnp.einsum('bno,o->bn', h, a2)
        scores = jax.nn.leaky_relu(f1[:, :, None] + f2[:, None, :], negative_slope=ALPHA)
        scores = jnp.where(adj == 0, NEG_INF, scores)
        attn = jax.nn.softmax(scores, axis=2)
        h_prime = jnp.einsum('bnm,bmi->bni', attn, graph_input)
        return jax.nn.elu(h_prime)

    def _L3_gnn_ref(adj, x, W1, att_src1, att_dst1, b1, W2, att_src2, att_dst2, b2):
        import jax, jax.numpy as jnp
        import numpy as np
        NEG_INF = -1000000000.0
        NEG_SLOPE = 0.2

        def gat_layer(x, mask, W, a_src, a_dst, bias, concat):
            B, N, _ = x.shape
            H, F = a_src.shape
            xl = (x @ W).reshape(B, N, H, F)
            asrc = jnp.einsum('bnhf,hf->bnh', xl, a_src)
            adst = jnp.einsum('bnhf,hf->bnh', xl, a_dst)
            e = jax.nn.leaky_relu(asrc[:, :, None, :] + adst[:, None, :, :], NEG_SLOPE)
            e = jnp.where(mask[..., None], e, NEG_INF)
            attn = jax.nn.softmax(e, axis=1)
            out = jnp.einsum('bsdh,bshf->bdhf', attn, xl)
            if concat:
                out = out.reshape(B, N, H * F)
            else:
                out = out.mean(axis=2)
            return out + bias
        B, N, _ = adj.shape
        mask = (adj > 0) | jnp.eye(N, dtype=bool)[None]
        h = jax.nn.elu(gat_layer(x, mask, W1, att_src1, att_dst1, b1, concat=True))
        h = gat_layer(h, mask, W2, att_src2, att_dst2, b2, concat=False)
        return h

    h = jnp.maximum(_layernorm(x, axis=-1), 0.0)
    x = x + _L0_gnn_ref(h, L0_gnn_W, L0_gnn_a, adj)
    h = jnp.maximum(_layernorm(x, axis=-1), 0.0)
    x = x + _L1_gnn_ref(h, adj, L1_gnn_W, L1_gnn_a)
    h = jnp.maximum(_layernorm(x, axis=-1), 0.0)
    x = x + _L2_gnn_ref(h, adj, L2_gnn_W_fc, L2_gnn_W_attn)
    h = jnp.maximum(_layernorm(x, axis=-1), 0.0)
    x = x + _L3_gnn_ref(adj, h, L3_gnn_W1, L3_gnn_att_src1, L3_gnn_att_dst1, L3_gnn_b1, L3_gnn_W2, L3_gnn_att_src2, L3_gnn_att_dst2, L3_gnn_b2)
    return x


_drawn_inputs = setup_inputs


def setup_inputs(seed=0):
    import zlib

    import numpy as np

    out = dict(_drawn_inputs(seed))
    spreads = {}
    factors = {'L2_gnn_W_fc': 4.648,
     'L2_gnn_W_attn': 4.039,
     'L3_gnn_att_src1': 3.223,
     'L3_gnn_att_dst1': 8.0,
     'L3_gnn_att_src2': 8.0,
     'L3_gnn_att_dst2': 64.0}
    for name, (base, spread) in spreads.items():
        noise = np.random.default_rng([zlib.crc32(name.encode()), seed]).standard_normal(out[name].shape)
        drawn = base * np.exp(spread * noise) if base else spread * noise
        out[name] = jnp.asarray(drawn.astype(out[name].dtype))
    for name, factor in factors.items():
        out[name] = (out[name] * factor).astype(out[name].dtype)
    return out
```

```python
from contextlib import ExitStack

import concourse.bass as bass
from concourse import mybir

ALU = mybir.AluOpType
ACT = mybir.ActivationFunctionType
F32 = mybir.dt.float32
F32R = mybir.dt.float32r
I32 = mybir.dt.int32

P = 128
KSEL = 64
LOROW = 32
BIG = 1.0e30
EPS = 1e-5
SLOPE = 0.2
ROUNDS = 5


OLDEST = 5


class Graph:

    def __init__(self, engine, base, offset, values):
        self.engine, self.base, self.offset, self.values = engine, base, offset, values
        self.slot = offset % 2

    def has_past(self, back):
        return self.base is not None or self.offset >= back

    def value(self, more, unit):
        if self.base is None:
            return unit * (self.offset + more)
        key = (self.offset + more, unit)
        if key not in self.values:
            self.values[key] = self.engine.snap((self.base + (self.offset + more)) * unit)
        return self.values[key]

    def count(self, back=0):
        return self.value(1 - back, 1)

    def dma_count(self, back=0):
        return self.value(2 - back - self.slot, 8)

    def row(self, tensor):
        return tensor[self.offset if self.base is None else self.base + self.offset]


def in_turns(engine, graphs, turn):
    head = OLDEST + 2 + OLDEST % 2
    passes = (graphs - head) // 2
    tail = head + 2 * passes if passes > 0 else head

    def peeled(t):
        turn(*(Graph(engine, None, t - n, None) if 0 <= t - n < graphs else None for n in range(OLDEST + 1)))

    for t in range(head):
        peeled(t)
    if passes > 0:
        with engine.Fori(head, tail - 1, 2) as t0:
            values = {}
            for u in range(2):
                turn(*(Graph(engine, t0, u - n, values) for n in range(OLDEST + 1)))
    for t in range(tail, graphs + OLDEST):
        peeled(t)


def prepare_weights(nc, consts, dram):
    (eye, noteye, half, eps, sel_r, w_hi, w_lo, v_f, v_r, NV, bias3, bias4) = consts
    (w0, a0, w1, a1, wfc, afc, w3, as3, ad3, b3, w4, as4, ad4, b4, ident, sel) = dram
    H, FH = as3.shape
    F, HF = w3.shape
    O = wfc.shape[0]

    with ExitStack() as ctx:
        def sb(name, shape, dt=F32):
            return ctx.enter_context(nc.sbuf_tensor("setup_" + name, list(shape), dt))

        def sem(name):
            return ctx.enter_context(nc.semaphore("setup_" + name))

        w_f = [sb(f"w{r}", w_hi[r].shape) if w_hi[r] is not None else None for r in range(ROUNDS)]
        wfc_f = sb("wfc", [O, F])
        afc_f = sb("afc", [O, 2])
        sel_f = sb("sel", sel_r.shape)
        a_b = [sb(f"a{r}", [P, n]) if n else None for r, n in enumerate((2 * F, 2 * F, 0, 2 * HF, 2 * F))]
        junk = sb("junk", [P, F])
        vfc = ctx.enter_context(nc.psum_tensor("setup_vfc", [P, F // P, 2], F32))

        consts_loaded = sem("consts_loaded")
        w_loaded = [sem(f"w{r}_loaded") for r in range(ROUNDS)]
        a_loaded = sem("a_loaded")
        hi_ready, lo_ready = sem("hi_ready"), sem("lo_ready")
        dot_done, vfc_done = sem("dot_done"), sem("vfc_done")
        v_hi_ready, misc_done = sem("v_hi_ready"), sem("misc_done")
        pool_done = sem("pool_done")
        SPLIT = [r for r in range(ROUNDS) if w_hi[r] is not None]

        block = ctx.enter_context(nc.Block())

        @block.sync
        def _(sp):
            def row(v):
                return v.rearrange("(o n) -> o n", o=1)

            def load(dst, src, signal):
                sp.dma_start(dst, src).then_inc(signal, 16)

            w_dram = {0: w0, 1: w1, 3: w3, 4: w4}
            cols = {0: a0.rearrange("n x -> x n"), 1: a1.rearrange("n x -> x n")}
            for r in SPLIT:
                load(w_f[r][:], w_dram[r].rearrange("(c p) n -> p c n", p=P), w_loaded[r])
                if r == 0:
                    load(eye[:], ident, consts_loaded)
                    load(sel_f[:], sel, consts_loaded)
                    load(wfc_f[:], wfc, consts_loaded)
                    with nc.allow_non_contiguous_dma(reason="64 floats, once"):
                        load(afc_f[:], afc.rearrange("x (k o) -> o (x k)", k=2), consts_loaded)
                    load(bias3[:], row(b3).broadcast_to([P, HF]), consts_loaded)
                    load(bias4[:], row(b4).broadcast_to([P, F]), consts_loaded)
                if r in (0, 1):
                    load(a_b[r][:], cols[r].broadcast_to([P, 2 * F]), a_loaded)
                elif r == 3:
                    for k, a in enumerate((as3, ad3)):
                        load(a_b[r][:, k * HF:(k + 1) * HF], row(a.rearrange("h f -> (h f)")).broadcast_to([P, HF]), a_loaded)
                else:
                    for k, a in enumerate((as4, ad4)):
                        load(a_b[r][:, k * F:(k + 1) * F], a.broadcast_to([P, F]), a_loaded)

        @block.scalar
        def _(act):
            for n, r in enumerate(SPLIT):
                act.wait_ge(w_loaded[r], 16)
                act.activation(w_hi[r][:], w_f[r][:], ACT.Copy).then_inc(hi_ready, 1)
            for r in range(ROUNDS):
                act.wait_ge(dot_done, r + 1)
                act.activation(v_r[r][:, :, 0:NV[r]], v_f[r][:], ACT.Copy).then_inc(v_hi_ready, 1)

        @block.gpsimd
        def _(pool):
            pool.memset(half[:], -0.5)
            pool.memset(eps[:], EPS)
            pool.wait_ge(consts_loaded, 6 * 16)
            pool.tensor_scalar(noteye[:], eye[:], -1.0, 1.0, ALU.mult, ALU.add).then_inc(pool_done, 1)
            for n, r in enumerate(SPLIT):
                pool.wait_ge(hi_ready, n + 1)
                pool.tensor_tensor(w_lo[r][:], w_f[r][:], w_hi[r][:].bitcast(F32), ALU.subtract).then_inc(lo_ready, 1)

        @block.tensor
        def _(pe):
            pe.wait_ge(consts_loaded, 6 * 16)
            for c in range(F // P):
                mm = pe.matmul(vfc[:, c, :], wfc_f[:, c * P:(c + 1) * P], afc_f[:], start=True, stop=True)
            mm.then_inc(vfc_done, 1)

        @block.vector
        def _(dve):
            done = 0
            dve.wait_ge(a_loaded, 6 * 16)
            for r in range(ROUNDS):
                if r == 2:
                    dve.wait_ge(vfc_done, 1)
                    dve.tensor_scalar(v_f[r][:, :, 0], vfc[:, :, 1], -1.0, None, ALU.mult).then_inc(misc_done, 1)
                    dve.tensor_scalar(v_f[r][:, :, 1], vfc[:, :, 0], -1.0, None, ALU.mult).then_inc(misc_done, 1)
                    dve.wait_ge(misc_done, done + 2)
                    done += 2
                    dve.tensor_copy(v_f[r][:, 0, 0:1], v_f[r][:, 0, 0:1]).then_inc(dot_done, 1)
                    continue
                dve.wait_ge(w_loaded[r], 16)
                heads, width = (H, FH) if r == 3 else (1, F)
                for c in range(v_f[r].shape[1]):
                    for k in range(NV[r]):
                        half_, head = k // heads, k % heads
                        if r == 1:
                            half_ = 1 - half_
                        a = a_b[r][:, half_ * heads * width + head * width:][:, 0:width]
                        ins = dve.tensor_tensor_reduce(junk[:, 0:width], w_f[r][:, c, head * width:(head + 1) * width], a,
                                                       -1.0, 0.0, ALU.mult, ALU.add, v_f[r][:, c, k:k + 1])
                        last = c == v_f[r].shape[1] - 1 and k == NV[r] - 1
                        if last:
                            ins.then_inc(dot_done, 1)
                            dve.wait_ge(dot_done, r + 1)
                        else:
                            ins.then_inc(misc_done, 1)
                            done += 1
                            dve.wait_ge(misc_done, done)
            for r in range(ROUNDS):
                dve.wait_ge(v_hi_ready, r + 1)
                dve.tensor_tensor(v_r[r][:, :, NV[r]:2 * NV[r]], v_f[r][:], v_r[r][:, :, 0:NV[r]].bitcast(F32), ALU.subtract)
            dve.wait_ge(consts_loaded, 6 * 16)
            dve.tensor_copy(sel_r[:], sel_f[:])
            dve.tensor_scalar(bias4[:], bias4[:], -2.0, None, ALU.add)


def gat_layers_kernel(nc, x, adj, w0, a0, w1, a1, wfc, afc, w3, as3, ad3, b3, w4, as4, ad4, b4,
                      ident, sel, out):
    B, N, F = x.shape
    H, FH = as3.shape
    HF = H * FH
    C = F // P
    C4 = HF // P
    assert N == P and F == 512 and HF == 2 * F and H == 4

    with ExitStack() as ctx:
        def sb(name, shape, dt=F32):
            return ctx.enter_context(nc.sbuf_tensor("sb_" + name, shape, dt))

        def bank(name):
            return ctx.enter_context(nc.psum_tensor("ps_" + name, [P, F], F32))

        def sem(name):
            return ctx.enter_context(nc.semaphore(name))

        eye, noteye = sb("eye", [P, P]), sb("noteye", [P, P])
        half = sb("half", [P, 1])
        eps = sb("eps", [P, 1])
        sel_r = sb("sel_r", [KSEL, 2 + 2 * H, P], F32R)
        W_SHAPE = [[P, C, F], [P, C, F], None, [P, C, HF], [P, C4, F]]
        w_hi = [sb(f"w{r}_hi", s, F32R) if s else None for r, s in enumerate(W_SHAPE)]
        w_lo = [sb(f"w{r}_lo", s, F32R) if s else None for r, s in enumerate(W_SHAPE)]
        NV = [2, 2, 2, 2 * H, 2]
        CH = [C, C, C, C, C4]
        v_f = [sb(f"v{r}_f", [P, CH[r], NV[r]]) for r in range(ROUNDS)]
        v_r = [sb(f"v{r}_r", [P, CH[r], 2 * NV[r]], F32R) for r in range(ROUNDS)]
        bias3 = sb("bias3", [P, HF])
        bias4 = sb("bias4", [P, F])

        prepare_weights(nc, (eye, noteye, half, eps, sel_r, w_hi, w_lo, v_f, v_r, NV, bias3, bias4),
                        (w0, a0, w1, a1, wfc, afc, w3, as3, ad3, b3, w4, as4, ad4, b4, ident, sel))

        x_in = sb("x_in", [P, 2, F])
        x_mid = [sb(f"x_mid{r}", [P, 2, F]) for r in range(3)]
        x_out = sb("x_out", [P, 2, F])
        adj_i = sb("adj_i", [P, 2, P], I32)
        m_nat = sb("m_nat", [P, 2, P])
        m_le0 = sb("m_le0", [P, P])
        m_t = sb("m_t", [P, 2, P])
        m_self = sb("m_self", [P, 2, P])
        h4_hi = sb("h4_hi", [P, 2, C4 * P], F32R)
        h4_lo = sb("h4_lo", [P, 2, C4 * P], F32R)

        CHAIN = [0, 0, 1, 2, 3]

        def per_chain(name, shapes, dt=F32):
            return [sb(f"{name}_c{k}", s, dt) if s else None for k, s in enumerate(shapes)]

        HEADS = [1, 1, H, 1]
        st = per_chain("st", [[P, 6]] * 3)
        mv = per_chain("mv", [[P, 2]] * 3)
        ve = per_chain("ve", [[P, 1]] * 3)
        rstd = per_chain("rstd", [[P, 1]] * 3)
        xn = per_chain("xn", [[P, F]] * 3)
        hT_hi = per_chain("hT_hi", [[P, F]] * 3, F32R)
        hT_lo = per_chain("hT_lo", [[P, F]] * 3, F32R)
        h_nat = sb("h_nat", [P, F])
        rows_r = per_chain("rows_r", [[KSEL, P]] * 4, F32R)
        sc = per_chain("sc", [[P, n, P] for n in HEADS])
        mn = per_chain("mn", [[P, n] for n in HEADS])
        sm = per_chain("sm", [[P, n] for n in HEADS])
        rc = per_chain("rc", [[P, n] for n in HEADS])
        att = per_chain("att", [[P, n, P] for n in HEADS])
        val = per_chain("val", [[P, F], None, [P, HF], [P, F]])
        tmp = per_chain("tmp", [[P, 1, F], [P, 1, F], [P, 2, F], None])
        tmp2 = per_chain("tmp2", [[P, 1, F], [P, 1, F], [P, 2, F], None])

        serial = [bank(f"serial{k}") for k in range(4)]
        prod = [[bank("prod0")], None, [bank("prod2a"), bank("prod2b")], [bank("prod3")]]

        def per_round(name, rounds=range(ROUNDS)):
            return [sem(f"{name}{r}") if r in rounds else None for r in range(ROUNDS)]

        LN = range(4)
        x_loaded = [sem("x_loaded0"), sem("x_loaded1")]
        adj_loaded = [sem("adj_loaded0"), sem("adj_loaded1")]
        out_stored = [sem("out_stored0"), sem("out_stored1")]
        m_nat_ready, m_le0_ready, m_le0_turned = sem("m_nat_ready"), sem("m_le0_ready"), sem("m_le0_turned")
        m_t_ready, m_self_ready = sem("m_t_ready"), sem("m_self_ready")
        stats_done = per_round("stats_done", LN)
        moments_ready = per_round("moments_ready", LN)
        vareps_ready = per_round("vareps_ready", LN)
        rstd_ready = per_round("rstd_ready", LN)
        xn_ready = per_round("xn_ready", LN)
        h_nat_ready = sem("h_nat_ready")
        hT_turned = per_round("hT_turned", LN)
        hi_ready = per_round("hi_ready", LN)
        lo_ready = per_round("lo_ready", LN)
        rows_done = per_round("rows_done")
        rows_hi_ready = per_round("rows_hi_ready")
        rows_lo_ready = per_round("rows_lo_ready")
        z_done = per_round("z_done")
        z_copied = per_round("z_copied")
        leaky_done = per_round("leaky_done")
        max_done = per_round("max_done")
        exp_done = per_round("exp_done")
        recip_done = per_round("recip_done")
        norm_done = per_round("norm_done")
        att_turned = per_round("att_turned", range(1, 5))
        att_ready = per_round("att_ready", range(1, 5))
        prod_done = per_round("prod_done", (0, 1, 3, 4))
        val_ready = per_round("val_ready", (0, 1, 3, 4))
        prod3b_done, val3b_ready = sem("prod3b_done"), sem("val3b_ready")
        mix_done = per_round("mix_done")
        neg_ready = per_round("neg_ready", range(3))
        elu_exp_ready = per_round("elu_exp_ready", (1, 2))
        resid_ready = per_round("resid_ready", range(3))
        x_ready = per_round("x_ready", (0, 1, 2, 4))
        mix3_done = [mix_done[3], sem("mix3b_done")]
        neg3_ready = [sem("neg3a_ready"), sem("neg3b_ready")]
        exp3_ready = [sem("exp3a_ready"), sem("exp3b_ready")]
        sum3_ready = [sem("sum3a_ready"), sem("sum3b_ready")]
        h4_hi_ready = [sem("h4_hi_a_ready"), sem("h4_hi_b_ready")]
        h4_lo_ready = [sem("h4_lo_a_ready"), sem("h4_lo_b_ready")]
        rows_cleared, wait_passed = sem("rows_cleared"), sem("wait_passed")

        block = ctx.enter_context(nc.Block())

        @block.sync
        def _(sp):
            def turn(g0, g1, g2, g3, g4, g5):
                if g0:
                    if g0.has_past(2):
                        sp.wait_ge(resid_ready[0], g0.count(back=2))
                    sp.dma_start(x_in[:, g0.slot, :], g0.row(x)).then_inc(x_loaded[g0.slot], 16)
                    if g0.has_past(2):
                        sp.wait_ge(m_nat_ready, g0.count(back=2))
                        sp.wait_ge(m_le0_ready, g0.count(back=2))
                    sp.dma_start(adj_i[:, g0.slot, :], g0.row(adj)).then_inc(adj_loaded[g0.slot], 16)
                if g5:
                    sp.wait_ge(x_ready[4], g5.count())
                    sp.dma_start(g5.row(out), x_out[:, g5.slot, :]).then_inc(out_stored[g5.slot], 16)

            in_turns(sp, B, turn)
            for slot in range(2):
                sp.wait_ge(out_stored[slot], 16 * len(range(slot, B, 2)))

        @block.tensor
        def _(pe):
            def score_rows(r, hi, lo):
                for c in range(CH[r]):
                    for part in (hi, lo):
                        mm = pe.matmul(serial[CHAIN[r]][0:2 * NV[r], 0:P], v_r[r][:, c, :], part[:, c * P:(c + 1) * P],
                                       start=(c == 0 and part is hi), stop=(c == CH[r] - 1 and part is lo))
                return mm

            def product(r, hi, lo, c, q=0):
                a, b = hi[:, c * P:(c + 1) * P], lo[:, c * P:(c + 1) * P]
                wh, wl = w_hi[r][:, c, q * F:(q + 1) * F], w_lo[r][:, c, q * F:(q + 1) * F]
                dst = prod[CHAIN[r]][q][:]
                pe.matmul(dst, a, wh, start=(c == 0), stop=False)
                pe.matmul(dst, a, wl, start=False, stop=False)
                return pe.matmul(dst, b, wh, start=False, stop=(c == CH[r] - 1))

            def scores(k, h, row, col):
                dst = serial[k][:, h * P:(h + 1) * P]
                pe.matmul(dst, sel_r[:, row, :], rows_r[k][:], start=True, stop=False)
                return pe.matmul(dst, rows_r[k][:], sel_r[:, col, :], start=False, stop=True)

            def turn(g0, g1, g2, g3, g4, g5):
                if g2:
                    pe.wait_ge(lo_ready[1], g2.count())
                    score_rows(1, hT_hi[0], hT_lo[0]).then_inc(rows_done[1], 1)
                if g2:
                    product(1, hT_hi[0], hT_lo[0], 0)
                if g2:
                    pe.wait_ge(rows_lo_ready[1], g2.count())
                    scores(0, 0, 0, 1).then_inc(z_done[1], 1)
                if g2:
                    for c in range(1, 4):
                        mm = product(1, hT_hi[0], hT_lo[0], c)
                    mm.then_inc(prod_done[1], 1)
                if g4:
                    pe.wait_ge(h4_hi_ready[0], g4.count())
                    pe.wait_ge(h4_lo_ready[0], g4.count())
                    pe.wait_ge(h4_hi_ready[1], g4.count())
                    pe.wait_ge(h4_lo_ready[1], g4.count())
                    if g4.has_past(1):
                        pe.wait_ge(x_ready[4], g4.count(back=1))
                    score_rows(4, h4_hi[:, g4.slot], h4_lo[:, g4.slot]).then_inc(rows_done[4], 1)
                if g2:
                    pe.wait_ge(norm_done[1], g2.count())
                    pe.transpose(serial[0][:, 0:P], sc[0][:, 0, :], eye[:]).then_inc(att_turned[1], 1)
                if g4:
                    if g4.has_past(1):
                        pe.wait_ge(val_ready[4], g4.count(back=1))
                    product(4, h4_hi[:, g4.slot], h4_lo[:, g4.slot], 0)
                if g2:
                    pe.wait_ge(att_ready[1], g2.count())
                    pe.wait_ge(val_ready[1], g2.count())
                    pe.matmul(serial[0][:], att[0][:, 0, :], val[0][:], start=True, stop=True).then_inc(mix_done[1], 1)
                if g4:
                    for c in range(1, 3):
                        mm = product(4, h4_hi[:, g4.slot], h4_lo[:, g4.slot], c)
                if g3:
                    pe.wait_ge(xn_ready[3], g3.count())
                    for c in range(C):
                        mm = pe.transpose(serial[2][:, c * P:(c + 1) * P], xn[2][:, c * P:(c + 1) * P], eye[:])
                    mm.then_inc(hT_turned[3], 1)
                if g4:
                    product(4, h4_hi[:, g4.slot], h4_lo[:, g4.slot], 3)
                if g4:
                    pe.wait_ge(rows_lo_ready[4], g4.count())
                    scores(3, 0, 0, 1).then_inc(z_done[4], 1)
                if g4:
                    product(4, h4_hi[:, g4.slot], h4_lo[:, g4.slot], 4)
                if g3:
                    pe.wait_ge(lo_ready[3], g3.count())
                    score_rows(3, hT_hi[2], hT_lo[2]).then_inc(rows_done[3], 1)
                if g4:
                    product(4, h4_hi[:, g4.slot], h4_lo[:, g4.slot], 5)
                if g3:
                    if g3.has_past(1):
                        pe.wait_ge(sum3_ready[0], g3.count(back=1))
                    product(3, hT_hi[2], hT_lo[2], 0, q=0)
                if g4:
                    product(4, h4_hi[:, g4.slot], h4_lo[:, g4.slot], 6)
                if g1:
                    pe.wait_ge(m_le0_ready, g1.count())
                    if g1.has_past(1):
                        pe.wait_ge(x_ready[1], g1.count(back=1))
                    pe.transpose(serial[0][:, 0:P], m_le0[:], eye[:]).then_inc(m_le0_turned, 1)
                if g3:
                    product(3, hT_hi[2], hT_lo[2], 1, q=0)
                if g1:
                    pe.wait_ge(xn_ready[0], g1.count())
                    pe.wait_ge(m_t_ready, g1.count())
                    for c in range(C):
                        mm = pe.transpose(serial[0][:, c * P:(c + 1) * P], xn[0][:, c * P:(c + 1) * P], eye[:])
                    mm.then_inc(hT_turned[0], 1)
                if g3:
                    pe.wait_ge(rows_lo_ready[3], g3.count())
                    for h in range(H):
                        mm = scores(2, h, 2 + h, 2 + H + h)
                    mm.then_inc(z_done[3], 1)
                if g4:
                    product(4, h4_hi[:, g4.slot], h4_lo[:, g4.slot], 7).then_inc(prod_done[4], 1)
                if g1:
                    pe.wait_ge(lo_ready[0], g1.count())
                    score_rows(0, hT_hi[0], hT_lo[0]).then_inc(rows_done[0], 1)
                if g3:
                    product(3, hT_hi[2], hT_lo[2], 2, q=0)
                if g2:
                    pe.wait_ge(h_nat_ready, g2.count())
                    for c in range(C):
                        mm = pe.transpose(serial[1][:, c * P:(c + 1) * P], h_nat[:, c * P:(c + 1) * P], eye[:])
                    mm.then_inc(hT_turned[2], 1)
                if g1:
                    product(0, hT_hi[0], hT_lo[0], 0)
                if g1:
                    pe.wait_ge(rows_lo_ready[0], g1.count())
                    scores(0, 0, 0, 1).then_inc(z_done[0], 1)
                if g1:
                    product(0, hT_hi[0], hT_lo[0], 1)
                if g3:
                    product(3, hT_hi[2], hT_lo[2], 3, q=0).then_inc(prod_done[3], 1)
                if g1:
                    for c in range(2, 4):
                        mm = product(0, hT_hi[0], hT_lo[0], c)
                    mm.then_inc(prod_done[0], 1)
                if g3:
                    if g3.has_past(1):
                        pe.wait_ge(sum3_ready[1], g3.count(back=1))
                    product(3, hT_hi[2], hT_lo[2], 0, q=1)
                if g1:
                    pe.wait_ge(norm_done[0], g1.count())
                    pe.wait_ge(val_ready[0], g1.count())
                    pe.matmul(serial[0][:], att[0][:, 0, :], val[0][:], start=True, stop=True).then_inc(mix_done[0], 1)
                if g3:
                    product(3, hT_hi[2], hT_lo[2], 1, q=1)
                if g2:
                    pe.wait_ge(lo_ready[2], g2.count())
                    score_rows(2, hT_hi[1], hT_lo[1]).then_inc(rows_done[2], 1)
                if g3:
                    product(3, hT_hi[2], hT_lo[2], 2, q=1)
                if g4:
                    pe.wait_ge(norm_done[4], g4.count())
                    pe.transpose(serial[3][:, 0:P], sc[3][:, 0, :], eye[:]).then_inc(att_turned[4], 1)
                if g3:
                    pe.wait_ge(norm_done[3], g3.count())
                    for h in range(H):
                        mm = pe.transpose(serial[2][:, h * P:(h + 1) * P], sc[2][:, h, :], eye[:])
                    mm.then_inc(att_turned[3], 1)
                if g3:
                    product(3, hT_hi[2], hT_lo[2], 3, q=1).then_inc(prod3b_done, 1)
                if g2:
                    pe.wait_ge(rows_lo_ready[2], g2.count())
                    scores(1, 0, 0, 1).then_inc(z_done[2], 1)
                if g3:
                    pe.wait_ge(att_ready[3], g3.count())
                    pe.wait_ge(val_ready[3], g3.count())
                    for f in range(C):
                        mm = pe.matmul(prod[2][0][:, f % C * P:(f % C + 1) * P], val[2][:, f * P:(f + 1) * P],
                                       att[2][:, f * P // FH, :], start=True, stop=True)
                    mm.then_inc(mix3_done[0], 1)
                if g4:
                    pe.wait_ge(att_ready[4], g4.count())
                    pe.wait_ge(val_ready[4], g4.count())
                    pe.matmul(serial[3][:], att[3][:, 0, :], val[3][:], start=True, stop=True).then_inc(mix_done[4], 1)
                if g3:
                    pe.wait_ge(att_ready[3], g3.count())
                    pe.wait_ge(val3b_ready, g3.count())
                    for f in range(C, 2 * C):
                        mm = pe.matmul(prod[2][1][:, f % C * P:(f % C + 1) * P], val[2][:, f * P:(f + 1) * P],
                                       att[2][:, f * P // FH, :], start=True, stop=True)
                    mm.then_inc(mix3_done[1], 1)
                if g1:
                    pe.wait_ge(xn_ready[1], g1.count())
                    for c in range(C):
                        mm = pe.transpose(serial[0][:, c * P:(c + 1) * P], xn[0][:, c * P:(c + 1) * P], eye[:])
                    mm.then_inc(hT_turned[1], 1)
                if g2:
                    pe.wait_ge(norm_done[2], g2.count())
                    pe.transpose(serial[1][:, 0:P], sc[1][:, 0, :], eye[:]).then_inc(att_turned[2], 1)
                if g2:
                    pe.wait_ge(att_ready[2], g2.count())
                    pe.matmul(serial[1][:], att[1][:, 0, :], h_nat[:], start=True, stop=True).then_inc(mix_done[2], 1)

            pe.wait_ge(rows_cleared, 4)
            in_turns(pe, B, turn)

        @block.scalar
        def _(act):
            def exp_rows(k, h):
                return act.activation(sc[k][:, h, :], sc[k][:, h, :], ACT.Exp, scale=-1.0,
                                      bias=mn[k][:, h:h + 1], accum_out=sm[k][:, h:h + 1])

            def turn(g0, g1, g2, g3, g4, g5):
                if g4:
                    act.wait_ge(mix3_done[1], g4.count())
                    act.activation(tmp[2][:, 1, :], prod[2][1][:], ACT.Relu, scale=-1.0).then_inc(neg3_ready[1], 1)
                    act.wait_ge(neg3_ready[1], g4.count())
                    act.activation(tmp[2][:, 1, :], tmp[2][:, 1, :], ACT.Exp, scale=-1.0).then_inc(exp3_ready[1], 1)
                if g4:
                    act.wait_ge(sum3_ready[0], g4.count())
                    if g4.has_past(2):
                        act.wait_ge(prod_done[4], g4.count(back=2))
                    act.activation(h4_hi[:, g4.slot, 0:F], tmp2[2][:, 0, :], ACT.Copy, bias=-1.0).then_inc(h4_hi_ready[0], 1)
                if g2:
                    act.wait_ge(rows_done[1], g2.count())
                    act.activation(rows_r[0][0:2 * NV[1], :], serial[0][0:2 * NV[1], 0:P], ACT.Copy).then_inc(rows_hi_ready[1], 1)
                if g3:
                    act.wait_ge(mix_done[2], g3.count())
                    act.activation(tmp[1][:, 0, :], serial[1][:], ACT.Relu, scale=-1.0).then_inc(neg_ready[2], 1)
                    act.wait_ge(neg_ready[2], g3.count())
                    act.activation(tmp[1][:, 0, :], tmp[1][:, 0, :], ACT.Exp, scale=-1.0).then_inc(elu_exp_ready[2], 1)
                if g2:
                    act.wait_ge(z_done[1], g2.count())
                    act.activation(sc[0][:].rearrange("p h n -> p (h n)"), serial[0][:, 0:P], ACT.Copy).then_inc(z_copied[1], 1)
                if g4:
                    act.wait_ge(sum3_ready[1], g4.count())
                    if g4.has_past(2):
                        act.wait_ge(prod_done[4], g4.count(back=2))
                    act.activation(h4_hi[:, g4.slot, F:2 * F], tmp2[2][:, 1, :], ACT.Copy, bias=-1.0).then_inc(h4_hi_ready[1], 1)
                if g2:
                    act.wait_ge(max_done[1], g2.count())
                    exp_rows(0, 0).then_inc(exp_done[1], 1)
                if g2:
                    act.wait_ge(prod_done[1], g2.count())
                    act.activation(val[0][:], prod[0][0][:], ACT.Copy).then_inc(val_ready[1], 1)
                if g2:
                    act.wait_ge(att_turned[1], g2.count())
                    act.activation(att[0][:].rearrange("p h n -> p (h n)"), serial[0][:, 0:P], ACT.Copy).then_inc(att_ready[1], 1)
                if g4:
                    act.wait_ge(rows_done[4], g4.count())
                    act.activation(rows_r[3][0:2 * NV[4], :], serial[3][0:2 * NV[4], 0:P], ACT.Copy).then_inc(rows_hi_ready[4], 1)
                if g2:
                    act.wait_ge(mix_done[1], g2.count())
                    act.activation(tmp[0][:, 0, :], serial[0][:], ACT.Relu, scale=-1.0).then_inc(neg_ready[1], 1)
                    act.wait_ge(neg_ready[1], g2.count())
                    act.activation(tmp[0][:, 0, :], tmp[0][:, 0, :], ACT.Exp, scale=-1.0).then_inc(elu_exp_ready[1], 1)
                if g3:
                    act.wait_ge(hT_turned[3], g3.count())
                    act.activation(hT_hi[2][:], serial[2][:], ACT.Relu).then_inc(hi_ready[3], 1)
                if g3:
                    act.wait_ge(rows_done[3], g3.count())
                    act.activation(rows_r[2][0:2 * NV[3], :], serial[2][0:2 * NV[3], 0:P], ACT.Copy).then_inc(rows_hi_ready[3], 1)
                if g1:
                    act.wait_ge(m_le0_turned, g1.count())
                    if g1.has_past(2):
                        act.wait_ge(max_done[0], g1.count(back=2))
                    if g1.has_past(2):
                        act.wait_ge(m_self_ready, g1.count(back=2))
                    act.activation(m_t[:, g1.slot, :], serial[0][:, 0:P], ACT.Copy).then_inc(m_t_ready, 1)
                if g4:
                    act.wait_ge(z_done[4], g4.count())
                    act.activation(sc[3][:].rearrange("p h n -> p (h n)"), serial[3][:, 0:P], ACT.Copy).then_inc(z_copied[4], 1)
                if g1:
                    act.wait_ge(hT_turned[0], g1.count())
                    act.activation(hT_hi[0][:], serial[0][:], ACT.Relu).then_inc(hi_ready[0], 1)
                if g3:
                    act.wait_ge(z_done[3], g3.count())
                    act.activation(sc[2][:].rearrange("p h n -> p (h n)"), serial[2][:, 0:H * P], ACT.Copy).then_inc(z_copied[3], 1)
                if g2:
                    act.wait_ge(xn_ready[2], g2.count())
                    act.activation(h_nat[:], xn[1][:], ACT.Relu).then_inc(h_nat_ready, 1)
                if g1:
                    act.wait_ge(rows_done[0], g1.count())
                    act.activation(rows_r[0][0:2 * NV[0], :], serial[0][0:2 * NV[0], 0:P], ACT.Copy).then_inc(rows_hi_ready[0], 1)
                if g2:
                    act.wait_ge(hT_turned[2], g2.count())
                    act.activation(hT_hi[1][:], serial[1][:], ACT.Relu).then_inc(hi_ready[2], 1)
                if g1:
                    act.wait_ge(z_done[0], g1.count())
                    act.activation(sc[0][:].rearrange("p h n -> p (h n)"), serial[0][:, 0:P], ACT.Copy).then_inc(z_copied[0], 1)
                if g3:
                    act.wait_ge(max_done[3], g3.count())
                    for h in range(H):
                        ins = exp_rows(2, h)
                    ins.then_inc(exp_done[3], 1)
                if g1:
                    act.wait_ge(max_done[0], g1.count())
                    exp_rows(0, 0).then_inc(exp_done[0], 1)
                if g1:
                    act.wait_ge(prod_done[0], g1.count())
                    act.activation(val[0][:], prod[0][0][:], ACT.Copy).then_inc(val_ready[0], 1)
                if g4:
                    act.wait_ge(max_done[4], g4.count())
                    exp_rows(3, 0).then_inc(exp_done[4], 1)
                if g1:
                    act.wait_ge(mix_done[0], g1.count())
                    act.activation(tmp[0][:, 0, :], serial[0][:], ACT.Relu, scale=-SLOPE).then_inc(neg_ready[0], 1)
                if g2:
                    act.wait_ge(rows_done[2], g2.count())
                    act.activation(rows_r[1][0:2 * NV[2], :], serial[1][0:2 * NV[2], 0:P], ACT.Copy).then_inc(rows_hi_ready[2], 1)
                if g4:
                    act.wait_ge(att_turned[4], g4.count())
                    act.activation(att[3][:].rearrange("p h n -> p (h n)"), serial[3][:, 0:P], ACT.Copy).then_inc(att_ready[4], 1)
                if g3:
                    act.wait_ge(att_turned[3], g3.count())
                    act.activation(att[2][:].rearrange("p h n -> p (h n)"), serial[2][:, 0:H * P], ACT.Copy).then_inc(att_ready[3], 1)
                if g2:
                    act.wait_ge(z_done[2], g2.count())
                    act.activation(sc[1][:].rearrange("p h n -> p (h n)"), serial[1][:, 0:P], ACT.Copy).then_inc(z_copied[2], 1)
                if g3:
                    act.wait_ge(mix3_done[0], g3.count())
                    act.activation(tmp[2][:, 0, :], prod[2][0][:], ACT.Relu, scale=-1.0).then_inc(neg3_ready[0], 1)
                    act.wait_ge(neg3_ready[0], g3.count())
                    act.activation(tmp[2][:, 0, :], tmp[2][:, 0, :], ACT.Exp, scale=-1.0).then_inc(exp3_ready[0], 1)
                if g2:
                    act.wait_ge(max_done[2], g2.count())
                    exp_rows(1, 0).then_inc(exp_done[2], 1)
                if g1:
                    act.wait_ge(hT_turned[1], g1.count())
                    act.activation(hT_hi[0][:], serial[0][:], ACT.Relu).then_inc(hi_ready[1], 1)
                if g2:
                    act.wait_ge(att_turned[2], g2.count())
                    act.activation(att[1][:].rearrange("p h n -> p (h n)"), serial[1][:, 0:P], ACT.Copy).then_inc(att_ready[2], 1)

            in_turns(act, B, turn)

        @block.gpsimd
        def _(pool):
            def turn(g0, g1, g2, g3, g4, g5):
                if g3:
                    pool.wait_ge(elu_exp_ready[2], g3.count())
                    pool.tensor_tensor(tmp2[1][:, 0, :], x_mid[1][:, g3.slot, :], tmp[1][:, 0, :], ALU.add).then_inc(resid_ready[2], 1)
                if g3:
                    pool.wait_ge(moments_ready[3], g3.count())
                    pool.tensor_tensor(ve[2][:], mv[2][:, 1:2], eps[:], ALU.add).then_inc(vareps_ready[3], 1)
                    pool.wait_ge(vareps_ready[3], g3.count())
                    pool.tensor_tensor(rstd[2][:], ve[2][:], half[:], ALU.pow).then_inc(rstd_ready[3], 1)
                if g2:
                    pool.wait_ge(elu_exp_ready[1], g2.count())
                    pool.tensor_tensor(tmp2[0][:, 0, :], x_mid[0][:, g2.slot, :], tmp[0][:, 0, :], ALU.add).then_inc(resid_ready[1], 1)
                if g1:
                    pool.wait_ge(moments_ready[0], g1.count())
                    pool.tensor_tensor(ve[0][:], mv[0][:, 1:2], eps[:], ALU.add).then_inc(vareps_ready[0], 1)
                    pool.wait_ge(vareps_ready[0], g1.count())
                    pool.tensor_tensor(rstd[0][:], ve[0][:], half[:], ALU.pow).then_inc(rstd_ready[0], 1)
                if g2:
                    pool.wait_ge(moments_ready[2], g2.count())
                    pool.tensor_tensor(ve[1][:], mv[1][:, 1:2], eps[:], ALU.add).then_inc(vareps_ready[2], 1)
                    pool.wait_ge(vareps_ready[2], g2.count())
                    pool.tensor_tensor(rstd[1][:], ve[1][:], half[:], ALU.pow).then_inc(rstd_ready[2], 1)
                if g3:
                    pool.wait_ge(m_t_ready, g3.count())
                    if g3.has_past(2):
                        pool.wait_ge(max_done[3], g3.count(back=2))
                    if g3.has_past(2):
                        pool.wait_ge(max_done[4], g3.count(back=2))
                    pool.tensor_tensor(m_self[:, g3.slot, :], m_t[:, g3.slot, :], noteye[:], ALU.mult).then_inc(m_self_ready, 1)
                if g3:
                    pool.wait_ge(recip_done[3], g3.count())
                    pool.tensor_tensor(sc[2][:], sc[2][:], rc[2][:].rearrange("p (h o) -> p h o", o=1).broadcast_to([P, H, P]),
                                       ALU.mult).then_inc(norm_done[3], 1)
                if g1:
                    pool.wait_ge(neg_ready[0], g1.count())
                    pool.tensor_tensor(tmp2[0][:, 0, :], x_in[:, g1.slot, :], tmp[0][:, 0, :], ALU.subtract).then_inc(resid_ready[0], 1)
                if g1:
                    pool.wait_ge(moments_ready[1], g1.count())
                    pool.tensor_tensor(ve[0][:], mv[0][:, 1:2], eps[:], ALU.add).then_inc(vareps_ready[1], 1)
                    pool.wait_ge(vareps_ready[1], g1.count())
                    pool.tensor_tensor(rstd[0][:], ve[0][:], half[:], ALU.pow).then_inc(rstd_ready[1], 1)

            in_turns(pool, B, turn)

        @block.vector
        def _(dve):
            def masked_min(k, h, mask):
                return dve.tensor_tensor_reduce(sc[k][:, h, :], sc[k][:, h, :], mask, 1.0, 3.0e38,
                                                ALU.add, ALU.min, mn[k][:, h:h + 1])

            def turn(g0, g1, g2, g3, g4, g5):
                if g2:
                    dve.wait_ge(hi_ready[1], g2.count())
                    dve.scalar_tensor_tensor(out=hT_lo[0][:], in0=serial[0][:], scalar=0.0, in1=hT_hi[0][:].bitcast(F32),
                                             op0=ALU.max, op1=ALU.subtract).then_inc(lo_ready[1], 1)
                if g5:
                    dve.wait_ge(mix_done[4], g5.count())
                    if g5.has_past(2):
                        dve.wait_ge(out_stored[g5.slot], g5.dma_count(back=2))
                    dve.tensor_tensor(x_out[:, g5.slot, :], serial[3][:], x_mid[2][:, g5.slot, :], ALU.add).then_inc(x_ready[4], 1)
                if g4:
                    dve.wait_ge(exp3_ready[1], g4.count())
                    dve.scalar_tensor_tensor(out=tmp2[2][:, 1, :], in0=prod[2][1][:], scalar=0.0, in1=tmp[2][:, 1, :],
                                             op0=ALU.max, op1=ALU.add).then_inc(sum3_ready[1], 1)
                if g1:
                    dve.wait_ge(adj_loaded[g1.slot], g1.dma_count())
                    dve.tensor_scalar(m_nat[:, g1.slot, :], adj_i[:, g1.slot, :], 0, BIG, ALU.is_equal, ALU.mult).then_inc(m_nat_ready, 1)
                    if g1.has_past(1):
                        dve.wait_ge(m_le0_turned, g1.count(back=1))
                    dve.tensor_scalar(m_le0[:], adj_i[:, g1.slot, :], 0, BIG, ALU.is_le, ALU.mult).then_inc(m_le0_ready, 1)
                if g2:
                    dve.wait_ge(rows_hi_ready[1], g2.count())
                    dve.tensor_tensor(rows_r[0][LOROW:LOROW + 2 * NV[1], :], serial[0][0:2 * NV[1], 0:P], rows_r[0][0:2 * NV[1], :].bitcast(F32),
                                      ALU.subtract).then_inc(rows_lo_ready[1], 1)
                if g4:
                    dve.wait_ge(h4_hi_ready[0], g4.count())
                    dve.scalar_tensor_tensor(out=h4_lo[:, g4.slot, 0:F], in0=tmp2[2][:, 0, :], scalar=-1.0,
                                             in1=h4_hi[:, g4.slot, 0:F].bitcast(F32),
                                             op0=ALU.add, op1=ALU.subtract).then_inc(h4_lo_ready[0], 1)
                if g2:
                    dve.wait_ge(z_copied[1], g2.count())
                    dve.scalar_tensor_tensor(out=sc[0][:], in0=sc[0][:], scalar=SLOPE, in1=sc[0][:],
                                             op0=ALU.mult, op1=ALU.min).then_inc(leaky_done[1], 1)
                    dve.wait_ge(leaky_done[1], g2.count())
                    dve.wait_ge(m_nat_ready, g2.count())
                    dve.sem_inc(wait_passed, 1)
                    masked_min(0, 0, m_nat[:, g2.slot, :]).then_inc(max_done[1], 1)
                if g4:
                    dve.wait_ge(h4_hi_ready[1], g4.count())
                    dve.scalar_tensor_tensor(out=h4_lo[:, g4.slot, F:2 * F], in0=tmp2[2][:, 1, :], scalar=-1.0,
                                             in1=h4_hi[:, g4.slot, F:2 * F].bitcast(F32),
                                             op0=ALU.add, op1=ALU.subtract).then_inc(h4_lo_ready[1], 1)
                if g2:
                    dve.wait_ge(exp_done[1], g2.count())
                    dve.reciprocal(rc[0][:], sm[0][:]).then_inc(recip_done[1], 1)
                    dve.wait_ge(recip_done[1], g2.count())
                    dve.tensor_scalar(sc[0][:, 0, :], sc[0][:, 0, :], rc[0][:], None, ALU.mult).then_inc(norm_done[1], 1)
                if g3:
                    dve.wait_ge(resid_ready[2], g3.count())
                    if g3.has_past(2):
                        dve.wait_ge(x_ready[4], g3.count(back=2))
                    dve.scalar_tensor_tensor(out=x_mid[2][:, g3.slot, :], in0=serial[1][:], scalar=0.0, in1=tmp2[1][:, 0, :],
                                             op0=ALU.max, op1=ALU.add).then_inc(x_ready[2], 1)
                if g3:
                    dve.wait_ge(x_ready[2], g3.count())
                    dve.bn_stats(st[2][:], x_mid[2][:, g3.slot, :]).then_inc(stats_done[3], 1)
                    dve.wait_ge(stats_done[3], g3.count())
                    dve.sem_inc(wait_passed, 1)
                    dve.bn_aggr(mv[2][:], st[2][:]).then_inc(moments_ready[3], 1)
                if g3:
                    dve.wait_ge(rstd_ready[3], g3.count())
                    dve.tensor_scalar(xn[2][:], x_mid[2][:, g3.slot, :], mv[2][:, 0:1], rstd[2][:], ALU.subtract, ALU.mult).then_inc(xn_ready[3], 1)
                if g4:
                    dve.wait_ge(rows_hi_ready[4], g4.count())
                    dve.tensor_tensor(rows_r[3][LOROW:LOROW + 2 * NV[4], :], serial[3][0:2 * NV[4], 0:P], rows_r[3][0:2 * NV[4], :].bitcast(F32),
                                      ALU.subtract).then_inc(rows_lo_ready[4], 1)
                if g3:
                    dve.wait_ge(hi_ready[3], g3.count())
                    dve.scalar_tensor_tensor(out=hT_lo[2][:], in0=serial[2][:], scalar=0.0, in1=hT_hi[2][:].bitcast(F32),
                                             op0=ALU.max, op1=ALU.subtract).then_inc(lo_ready[3], 1)
                if g2:
                    dve.wait_ge(resid_ready[1], g2.count())
                    if g2.has_past(2):
                        dve.wait_ge(resid_ready[2], g2.count(back=2))
                    dve.scalar_tensor_tensor(out=x_mid[1][:, g2.slot, :], in0=serial[0][:], scalar=0.0, in1=tmp2[0][:, 0, :],
                                             op0=ALU.max, op1=ALU.add).then_inc(x_ready[1], 1)
                if g1:
                    dve.wait_ge(x_loaded[g1.slot], g1.dma_count())
                    dve.bn_stats(st[0][:], x_in[:, g1.slot, :]).then_inc(stats_done[0], 1)
                    dve.wait_ge(stats_done[0], g1.count())
                    dve.sem_inc(wait_passed, 1)
                    dve.bn_aggr(mv[0][:], st[0][:]).then_inc(moments_ready[0], 1)
                if g2:
                    dve.wait_ge(x_ready[1], g2.count())
                    dve.bn_stats(st[1][:], x_mid[1][:, g2.slot, :]).then_inc(stats_done[2], 1)
                    dve.wait_ge(stats_done[2], g2.count())
                    dve.sem_inc(wait_passed, 1)
                    dve.bn_aggr(mv[1][:], st[1][:]).then_inc(moments_ready[2], 1)
                if g3:
                    dve.wait_ge(rows_hi_ready[3], g3.count())
                    dve.tensor_tensor(rows_r[2][LOROW:LOROW + 2 * NV[3], :], serial[2][0:2 * NV[3], 0:P], rows_r[2][0:2 * NV[3], :].bitcast(F32),
                                      ALU.subtract).then_inc(rows_lo_ready[3], 1)
                if g1:
                    dve.wait_ge(rstd_ready[0], g1.count())
                    dve.tensor_scalar(xn[0][:], x_in[:, g1.slot, :], mv[0][:, 0:1], rstd[0][:], ALU.subtract, ALU.mult).then_inc(xn_ready[0], 1)
                if g2:
                    dve.wait_ge(rstd_ready[2], g2.count())
                    dve.tensor_scalar(xn[1][:], x_mid[1][:, g2.slot, :], mv[1][:, 0:1], rstd[1][:], ALU.subtract, ALU.mult).then_inc(xn_ready[2], 1)
                if g1:
                    dve.wait_ge(hi_ready[0], g1.count())
                    dve.scalar_tensor_tensor(out=hT_lo[0][:], in0=serial[0][:], scalar=0.0, in1=hT_hi[0][:].bitcast(F32),
                                             op0=ALU.max, op1=ALU.subtract).then_inc(lo_ready[0], 1)
                if g3:
                    dve.wait_ge(z_copied[3], g3.count())
                    dve.scalar_tensor_tensor(out=sc[2][:], in0=sc[2][:], scalar=SLOPE, in1=sc[2][:],
                                             op0=ALU.mult, op1=ALU.min).then_inc(leaky_done[3], 1)
                    dve.wait_ge(leaky_done[3], g3.count())
                    dve.wait_ge(m_self_ready, g3.count())
                    dve.sem_inc(wait_passed, 1)
                    for h in range(H):
                        ins = masked_min(2, h, m_self[:, g3.slot, :])
                    ins.then_inc(max_done[3], 1)
                if g1:
                    dve.wait_ge(rows_hi_ready[0], g1.count())
                    dve.tensor_tensor(rows_r[0][LOROW:LOROW + 2 * NV[0], :], serial[0][0:2 * NV[0], 0:P], rows_r[0][0:2 * NV[0], :].bitcast(F32),
                                      ALU.subtract).then_inc(rows_lo_ready[0], 1)
                if g2:
                    dve.wait_ge(hi_ready[2], g2.count())
                    dve.scalar_tensor_tensor(out=hT_lo[1][:], in0=serial[1][:], scalar=0.0, in1=hT_hi[1][:].bitcast(F32),
                                             op0=ALU.max, op1=ALU.subtract).then_inc(lo_ready[2], 1)
                if g1:
                    dve.wait_ge(z_copied[0], g1.count())
                    dve.scalar_tensor_tensor(out=sc[0][:], in0=sc[0][:], scalar=SLOPE, in1=sc[0][:],
                                             op0=ALU.mult, op1=ALU.min).then_inc(leaky_done[0], 1)
                    dve.wait_ge(leaky_done[0], g1.count())
                    dve.wait_ge(m_t_ready, g1.count())
                    dve.sem_inc(wait_passed, 1)
                    masked_min(0, 0, m_t[:, g1.slot, :]).then_inc(max_done[0], 1)
                if g4:
                    dve.wait_ge(z_copied[4], g4.count())
                    dve.scalar_tensor_tensor(out=sc[3][:], in0=sc[3][:], scalar=SLOPE, in1=sc[3][:],
                                             op0=ALU.mult, op1=ALU.min).then_inc(leaky_done[4], 1)
                    dve.wait_ge(leaky_done[4], g4.count())
                    dve.wait_ge(m_self_ready, g4.count())
                    dve.sem_inc(wait_passed, 1)
                    masked_min(3, 0, m_self[:, g4.slot, :]).then_inc(max_done[4], 1)
                if g3:
                    dve.wait_ge(exp_done[3], g3.count())
                    dve.reciprocal(rc[2][:], sm[2][:]).then_inc(recip_done[3], 1)
                if g1:
                    dve.wait_ge(exp_done[0], g1.count())
                    dve.reciprocal(rc[0][:], sm[0][:]).then_inc(recip_done[0], 1)
                    dve.wait_ge(recip_done[0], g1.count())
                    dve.tensor_scalar(att[0][:, 0, :], sc[0][:, 0, :], rc[0][:], None, ALU.mult).then_inc(norm_done[0], 1)
                if g4:
                    dve.wait_ge(prod_done[4], g4.count())
                    dve.tensor_tensor(val[3][:], prod[3][0][:], bias4[:], ALU.add).then_inc(val_ready[4], 1)
                if g4:
                    dve.wait_ge(exp_done[4], g4.count())
                    dve.reciprocal(rc[3][:], sm[3][:]).then_inc(recip_done[4], 1)
                    dve.wait_ge(recip_done[4], g4.count())
                    dve.tensor_scalar(sc[3][:, 0, :], sc[3][:, 0, :], rc[3][:], None, ALU.mult).then_inc(norm_done[4], 1)
                if g3:
                    dve.wait_ge(prod_done[3], g3.count())
                    dve.tensor_tensor(val[2][:, 0:F], prod[2][0][:], bias3[:, 0:F], ALU.add).then_inc(val_ready[3], 1)
                if g2:
                    dve.wait_ge(rows_hi_ready[2], g2.count())
                    dve.tensor_tensor(rows_r[1][LOROW:LOROW + 2 * NV[2], :], serial[1][0:2 * NV[2], 0:P], rows_r[1][0:2 * NV[2], :].bitcast(F32),
                                      ALU.subtract).then_inc(rows_lo_ready[2], 1)
                if g1:
                    dve.wait_ge(resid_ready[0], g1.count())
                    dve.scalar_tensor_tensor(out=x_mid[0][:, g1.slot, :], in0=serial[0][:], scalar=0.0, in1=tmp2[0][:, 0, :],
                                             op0=ALU.max, op1=ALU.add).then_inc(x_ready[0], 1)
                if g1:
                    dve.wait_ge(x_ready[0], g1.count())
                    dve.bn_stats(st[0][:], x_mid[0][:, g1.slot, :]).then_inc(stats_done[1], 1)
                    dve.wait_ge(stats_done[1], g1.count())
                    dve.sem_inc(wait_passed, 1)
                    dve.bn_aggr(mv[0][:], st[0][:]).then_inc(moments_ready[1], 1)
                if g3:
                    dve.wait_ge(prod3b_done, g3.count())
                    dve.tensor_tensor(val[2][:, F:2 * F], prod[2][1][:], bias3[:, F:2 * F], ALU.add).then_inc(val3b_ready, 1)
                if g2:
                    dve.wait_ge(z_copied[2], g2.count())
                    dve.scalar_tensor_tensor(out=sc[1][:], in0=sc[1][:], scalar=SLOPE, in1=sc[1][:],
                                             op0=ALU.mult, op1=ALU.min).then_inc(leaky_done[2], 1)
                    dve.wait_ge(leaky_done[2], g2.count())
                    dve.wait_ge(m_nat_ready, g2.count())
                    dve.sem_inc(wait_passed, 1)
                    masked_min(1, 0, m_nat[:, g2.slot, :]).then_inc(max_done[2], 1)
                if g1:
                    dve.wait_ge(rstd_ready[1], g1.count())
                    dve.tensor_scalar(xn[0][:], x_mid[0][:, g1.slot, :], mv[0][:, 0:1], rstd[0][:], ALU.subtract, ALU.mult).then_inc(xn_ready[1], 1)
                if g2:
                    dve.wait_ge(exp_done[2], g2.count())
                    dve.reciprocal(rc[1][:], sm[1][:]).then_inc(recip_done[2], 1)
                    dve.wait_ge(recip_done[2], g2.count())
                    dve.tensor_scalar(sc[1][:, 0, :], sc[1][:, 0, :], rc[1][:], None, ALU.mult).then_inc(norm_done[2], 1)
                if g3:
                    dve.wait_ge(exp3_ready[0], g3.count())
                    dve.scalar_tensor_tensor(out=tmp2[2][:, 0, :], in0=prod[2][0][:], scalar=0.0, in1=tmp[2][:, 0, :],
                                             op0=ALU.max, op1=ALU.add).then_inc(sum3_ready[0], 1)

            for k in range(4):
                dve.memset(rows_r[k][:].bitcast(F32), 0.0).then_inc(rows_cleared, 1)
            dve.wait_ge(rows_cleared, 4)
            in_turns(dve, B, turn)


def kernel(x, adj, L0_gnn_W, L0_gnn_a, L1_gnn_W, L1_gnn_a, L2_gnn_W_fc, L2_gnn_W_attn, L3_gnn_W1,
           L3_gnn_att_src1, L3_gnn_att_dst1, L3_gnn_b1, L3_gnn_W2, L3_gnn_att_src2, L3_gnn_att_dst2,
           L3_gnn_b2):
    import numpy as np
    import concourse.bacc as bacc
    from concourse.bass_utils import run_bass_kernel_spmd

    heads = L3_gnn_att_src1.shape[0]
    sel = np.zeros((KSEL, 2 + 2 * heads, P), np.float32)
    for part in (0, LOROW):
        for vec in range(2):
            for hl in range(2):
                sel[part + 2 * hl + vec, vec] = 1.0
                for h in range(heads):
                    sel[part + 2 * heads * hl + heads * vec + h, 2 + heads * vec + h] = 1.0
    named = dict(x=x, adj=adj, w0=L0_gnn_W, a0=L0_gnn_a, w1=L1_gnn_W, a1=L1_gnn_a, wfc=L2_gnn_W_fc,
                 afc=L2_gnn_W_attn, w3=L3_gnn_W1, as3=L3_gnn_att_src1, ad3=L3_gnn_att_dst1, b3=L3_gnn_b1,
                 w4=L3_gnn_W2, as4=L3_gnn_att_src2, ad4=L3_gnn_att_dst2, b4=L3_gnn_b2,
                 ident=np.eye(P, dtype=np.float32), sel=sel)
    nc = bacc.Bacc("TRN2", target_bir_lowering=False, num_devices=1)
    arrays, args = {}, {}
    for name, a in named.items():
        arrays[f"in_{name}"] = np.ascontiguousarray(a)
        args[name] = nc.dram_tensor(f"in_{name}", a.shape, mybir.dt.from_np(arrays[f"in_{name}"].dtype),
                                    kind="ExternalInput").ap()
    out = nc.dram_tensor("out", x.shape, F32, kind="ExternalOutput").ap()
    gat_layers_kernel(nc, out=out, **args)
    return run_bass_kernel_spmd(nc, [arrays], core_ids=[0]).results[0]["out"]
```

```python
from contextlib import ExitStack

import concourse.bass as bass
from concourse import mybir

ALU = mybir.AluOpType
ACT = mybir.ActivationFunctionType
F32 = mybir.dt.float32
F32R = mybir.dt.float32r
I32 = mybir.dt.int32

P = 128
KSEL = 64
LOROW = 32
BIG = 1.0e30
EPS = 1e-5
SLOPE = 0.2
ROUNDS = 5


OLDEST = 6


class Graph:

    def __init__(self, engine, base, offset, values, graphs):
        self.graphs = graphs
        self.engine, self.base, self.offset, self.values = engine, base, offset, values
        self.slot = offset % 2

    def has_past(self, back):
        return self.base is not None or self.offset >= back

    def has_next(self, ahead):
        return self.base is not None or self.offset + ahead < self.graphs

    def value(self, more, unit):
        if self.base is None:
            return unit * (self.offset + more)
        key = (self.offset + more, unit)
        if key not in self.values:
            self.values[key] = self.engine.snap((self.base + (self.offset + more)) * unit)
        return self.values[key]

    def count(self, back=0):
        return self.value(1 - back, 1)

    def dma_count(self, back=0):
        return self.value(2 - back - self.slot, 8)

    def row(self, tensor):
        return tensor[self.offset if self.base is None else self.base + self.offset]


def in_turns(engine, graphs, turn):
    head = OLDEST + 2 + OLDEST % 2
    passes = (graphs - head) // 2
    tail = head + 2 * passes if passes > 0 else head

    def peeled(t):
        turn(*(Graph(engine, None, t - n, None, graphs) if 0 <= t - n < graphs else None for n in range(OLDEST + 1)))

    for t in range(head):
        peeled(t)
    if passes > 0:
        with engine.Fori(head, tail - 1, 2) as t0:
            values = {}
            for u in range(2):
                turn(*(Graph(engine, t0, u - n, values, graphs) for n in range(OLDEST + 1)))
    for t in range(tail, graphs + OLDEST):
        peeled(t)


def prepare_weights(nc, consts, dram):
    (eye, noteye, half, eps, zero, sel_r, w_hi, w_lo, v_f, v_r, NV, bias3, bias4) = consts
    (w0, a0, w1, a1, wfc, afc, w3, as3, ad3, b3, w4, as4, ad4, b4, ident, sel) = dram
    H, FH = as3.shape
    F, HF = w3.shape
    O = wfc.shape[0]

    with ExitStack() as ctx:
        def sb(name, shape, dt=F32):
            return ctx.enter_context(nc.sbuf_tensor("setup_" + name, list(shape), dt))

        setup_sems = []

        def sem(name):
            setup_sems.append(nc.alloc_semaphore(name="setup_" + name))
            return setup_sems[-1]

        w_f = [sb(f"w{r}", w_hi[r].shape) if w_hi[r] is not None else None for r in range(ROUNDS)]
        wfc_f = sb("wfc", [O, F])
        afc_f = sb("afc", [O, 2])
        sel_f = sb("sel", sel_r.shape)
        a_b = [sb(f"a{r}", [P, n]) if n else None for r, n in enumerate((2 * F, 2 * F, 0, 2 * HF, 2 * F))]
        junk = sb("junk", [P, F])
        vfc = ctx.enter_context(nc.psum_tensor("setup_vfc", [P, F // P, 2], F32))

        consts_loaded, biases_loaded = sem("consts_loaded"), sem("biases_loaded")
        w_loaded = [sem(f"w{r}_loaded") for r in range(ROUNDS)]
        a_loaded = [sem(f"a{r}_loaded") for r in range(ROUNDS)]
        hi_ready, lo_ready = sem("hi_ready"), sem("lo_ready")
        dot_done, vfc_done = sem("dot_done"), sem("vfc_done")
        v_hi_ready, misc_done = sem("v_hi_ready"), sem("misc_done")
        pool_done = sem("pool_done")
        SPLIT = [r for r in range(ROUNDS) if w_hi[r] is not None]

        with nc.Block() as block:

            @block.sync
            def _(sp):
                def row(v):
                    return v.rearrange("(o n) -> o n", o=1)

                def load(dst, src, signal):
                    sp.dma_start(dst, src).then_inc(signal, 16)

                w_dram = {0: w0, 1: w1, 3: w3, 4: w4}
                cols = {0: a0.rearrange("n x -> x n"), 1: a1.rearrange("n x -> x n")}
                for r in SPLIT:
                    if r in (0, 1):
                        load(a_b[r][:], cols[r].broadcast_to([P, 2 * F]), a_loaded[r])
                    else:
                        for k, a in enumerate((as3, ad3) if r == 3 else (as4, ad4)):
                            n = HF if r == 3 else F
                            load(a_b[r][:, k * n:(k + 1) * n], row(a.rearrange("h f -> (h f)")).broadcast_to([P, n]), a_loaded[r])
                    load(w_f[r][:], w_dram[r].rearrange("(c p) n -> p c n", p=P), w_loaded[r])
                    if r == 0:
                        load(wfc_f[:], wfc, consts_loaded)
                        with nc.allow_non_contiguous_dma(reason="64 floats, once"):
                            load(afc_f[:], afc.rearrange("x (k o) -> o (x k)", k=2), consts_loaded)
                        load(eye[:], ident, consts_loaded)
                        load(sel_f[:], sel, consts_loaded)
                load(bias3[:], row(b3).broadcast_to([P, HF]), biases_loaded)
                load(bias4[:], row(b4).broadcast_to([P, F]), biases_loaded)

            @block.scalar
            def _(act):
                for n, r in enumerate(SPLIT):
                    act.wait_ge(w_loaded[r], 16)
                    act.activation(w_hi[r][:], w_f[r][:], ACT.Copy).then_inc(hi_ready, 1)
                for r in range(ROUNDS):
                    act.wait_ge(dot_done, r + 1)
                    act.activation(v_r[r][:, :, 0:NV[r]], v_f[r][:], ACT.Copy).then_inc(v_hi_ready, 1)

            @block.gpsimd
            def _(pool):
                pool.memset(half[:], -0.5)
                pool.memset(eps[:], EPS)
                pool.memset(zero[:], 0.0)
                pool.wait_ge(consts_loaded, 4 * 16)
                pool.tensor_scalar(noteye[:], eye[:], -1.0, 1.0, ALU.mult, ALU.add).then_inc(pool_done, 1)
                for n, r in enumerate(SPLIT):
                    pool.wait_ge(hi_ready, n + 1)
                    pool.tensor_tensor(w_lo[r][:], w_f[r][:], w_hi[r][:].bitcast(F32), ALU.subtract).then_inc(lo_ready, 1)

            @block.tensor
            def _(pe):
                pe.wait_ge(consts_loaded, 4 * 16)
                for c in range(F // P):
                    mm = pe.matmul(vfc[:, c, :], wfc_f[:, c * P:(c + 1) * P], afc_f[:], start=True, stop=True)
                mm.then_inc(vfc_done, 1)

            @block.vector
            def _(dve):
                done = 0
                for r in range(ROUNDS):
                    if r == 2:
                        dve.wait_ge(vfc_done, 1)
                        dve.tensor_scalar(v_f[r][:, :, 0], vfc[:, :, 1], -1.0, None, ALU.mult).then_inc(misc_done, 1)
                        dve.tensor_scalar(v_f[r][:, :, 1], vfc[:, :, 0], -1.0, None, ALU.mult).then_inc(misc_done, 1)
                        dve.wait_ge(misc_done, done + 2)
                        done += 2
                        dve.tensor_copy(v_f[r][:, 0, 0:1], v_f[r][:, 0, 0:1]).then_inc(dot_done, 1)
                        continue
                    dve.wait_ge(w_loaded[r], 16)
                    dve.wait_ge(a_loaded[r], 16 if r < 2 else 2 * 16)
                    heads, width = (H, FH) if r == 3 else (1, F)
                    for c in range(v_f[r].shape[1]):
                        for k in range(NV[r]):
                            half_, head = k // heads, k % heads
                            if r == 1:
                                half_ = 1 - half_
                            a = a_b[r][:, half_ * heads * width + head * width:][:, 0:width]
                            ins = dve.tensor_tensor_reduce(junk[:, 0:width], w_f[r][:, c, head * width:(head + 1) * width], a,
                                                           -1.0, 0.0, ALU.mult, ALU.add, v_f[r][:, c, k:k + 1])
                            last = c == v_f[r].shape[1] - 1 and k == NV[r] - 1
                            if last:
                                ins.then_inc(dot_done, 1)
                                dve.wait_ge(dot_done, r + 1)
                            else:
                                ins.then_inc(misc_done, 1)
                                done += 1
                                dve.wait_ge(misc_done, done)
                for r in range(ROUNDS):
                    dve.wait_ge(v_hi_ready, r + 1)
                    dve.tensor_tensor(v_r[r][:, :, NV[r]:2 * NV[r]], v_f[r][:], v_r[r][:, :, 0:NV[r]].bitcast(F32), ALU.subtract)
                dve.wait_ge(consts_loaded, 4 * 16)
                dve.tensor_copy(sel_r[:], sel_f[:])
                dve.wait_ge(biases_loaded, 2 * 16)
                dve.tensor_scalar(bias4[:], bias4[:], -2.0, None, ALU.add)

        nc.clear_and_free_semaphores(setup_sems)
        nc.all_engine_barrier()


def gat_layers_kernel(nc, x, adj, w0, a0, w1, a1, wfc, afc, w3, as3, ad3, b3, w4, as4, ad4, b4,
                      ident, sel, out):
    B, N, F = x.shape
    H, FH = as3.shape
    HF = H * FH
    C = F // P
    C4 = HF // P
    assert N == P and F == 512 and HF == 2 * F and H == 4

    with ExitStack() as ctx:
        def sb(name, shape, dt=F32):
            return ctx.enter_context(nc.sbuf_tensor("sb_" + name, shape, dt))

        def bank(name):
            return ctx.enter_context(nc.psum_tensor("ps_" + name, [P, F], F32))

        def sem(name):
            return ctx.enter_context(nc.semaphore(name))

        eye, noteye = sb("eye", [P, P]), sb("noteye", [P, P])
        half = sb("half", [P, 1])
        eps = sb("eps", [P, 1])
        zero = sb("zero", [P, 1])
        sel_r = sb("sel_r", [KSEL, 2 + 2 * H, P], F32R)
        W_SHAPE = [[P, C, F], [P, C, F], None, [P, C, HF], [P, C4, F]]
        w_hi = [sb(f"w{r}_hi", s, F32R) if s else None for r, s in enumerate(W_SHAPE)]
        w_lo = [sb(f"w{r}_lo", s, F32R) if s else None for r, s in enumerate(W_SHAPE)]
        NV = [2, 2, 2, 2 * H, 2]
        CH = [C, C, C, C, C4]
        v_f = [sb(f"v{r}_f", [P, CH[r], NV[r]]) for r in range(ROUNDS)]
        v_r = [sb(f"v{r}_r", [P, CH[r], 2 * NV[r]], F32R) for r in range(ROUNDS)]
        bias3 = sb("bias3", [P, HF])
        bias4 = sb("bias4", [P, F])

        prepare_weights(nc, (eye, noteye, half, eps, zero, sel_r, w_hi, w_lo, v_f, v_r, NV, bias3, bias4),
                        (w0, a0, w1, a1, wfc, afc, w3, as3, ad3, b3, w4, as4, ad4, b4, ident, sel))

        x_in = sb("x_in", [P, 2, F])
        x_mid = [sb(f"x_mid{r}", [P, 2, F]) for r in range(3)]
        x_out = sb("x_out", [P, 2, F])
        adj_i = sb("adj_i", [P, 2, P], I32)
        m_nat = sb("m_nat", [P, 2, P])
        m_le0 = sb("m_le0", [P, P])
        m_t = sb("m_t", [P, 2, P])
        m_self = sb("m_self", [P, 2, P])
        h4_hi = sb("h4_hi", [P, 2, C4 * P], F32R)
        h4_lo = sb("h4_lo", [P, 2, C4 * P], F32R)

        CHAIN = [0, 0, 1, 2, 3]

        def per_chain(name, shapes, dt=F32):
            return [sb(f"{name}_c{k}", s, dt) if s else None for k, s in enumerate(shapes)]

        HEADS = [1, 1, H, 1]
        st, mv, ve, nm, rstd = ([sb(f"{name}{r}", [P, n]) for r in range(4)] for name, n in (
            ("st", 6),
            ("mv", 2),
            ("ve", 1),
            ("nm", 1),
            ("rstd", 1)))
        xn = [sb(f"xn{r}", [P, F]) if r != 2 else None for r in range(4)]
        hT_hi = per_chain("hT_hi", [[P, F]] * 3, F32R)
        hT_lo = per_chain("hT_lo", [[P, F]] * 3, F32R)
        rows_r = per_chain("rows_r", [[KSEL, P]] * 4, F32R)
        sc = per_chain("sc", [[P, n, P] for n in HEADS])
        mn = per_chain("mn", [[P, n] for n in HEADS])
        sm = per_chain("sm", [[P, n] for n in HEADS])
        rc = per_chain("rc", [[P, n] for n in HEADS])
        att_hi = per_chain("att_hi", [[P, 1, P], [P, 1, P], None, [P, 1, P]], F32R)
        att_lo = per_chain("att_lo", [[P, 1, P], [P, 1, P], None, [P, 1, P]], F32R)
        att3 = sb("att3", [P, H, P])
        tmp = per_chain("tmp", [[P, 1, F], [P, 1, F], [P, 2, F], None])
        VAL = [[P, F], [P, F], None, [P, F]]
        val_hi = per_chain("val_hi", VAL, F32R)
        val_lo = per_chain("val_lo", VAL, F32R)
        val3 = sb("val3", [P, HF])
        val0_f, h_nat = tmp[0][:, 0, :], tmp[1][:, 0, :]

        serial = [bank(f"serial{k}") for k in range(4)]
        mixed = [bank("mixed0"), serial[3], serial[1], None, bank("mixed4")]
        mixed3 = [bank("mixed3a"), bank("mixed3b")]

        def per_round(name, rounds=range(ROUNDS)):
            return [sem(f"{name}{r}") if r in rounds else None for r in range(ROUNDS)]

        LN = range(4)
        x_loaded = [sem("x_loaded0"), sem("x_loaded1")]
        adj_loaded = [sem("adj_loaded0"), sem("adj_loaded1")]
        out_stored = [sem("out_stored0"), sem("out_stored1")]
        masks_ready, m_le0_turned = sem("masks_ready"), sem("m_le0_turned")
        m_t_ready, m_self_ready = sem("m_t_ready"), sem("m_self_ready")
        stats_done = per_round("stats_done", LN)
        moments_ready = per_round("moments_ready", LN)
        vareps_ready = per_round("vareps_ready", LN)
        rstd_done = per_round("rstd_done", LN)
        rstd_ready = per_round("rstd_ready", LN)
        xn_ready = per_round("xn_ready", (0, 1, 3))
        h_nat_ready = sem("h_nat_ready")
        hT_turned = per_round("hT_turned", LN)
        hi_ready = per_round("hi_ready", LN)
        lo_ready = per_round("lo_ready", LN)
        rows_done = per_round("rows_done")
        rows_hi_ready = per_round("rows_hi_ready")
        rows_lo_ready = per_round("rows_lo_ready")
        z_done = per_round("z_done")
        z_copied = per_round("z_copied")
        leaky_done = per_round("leaky_done")
        max_done = per_round("max_done")
        exp_done = per_round("exp_done")
        recip_done = per_round("recip_done")
        norm_done = per_round("norm_done", range(1, 5))
        att_turned = per_round("att_turned", range(1, 5))
        att_ready = per_round("att_ready", (3,))
        att_hi_ready = per_round("att_hi_ready", (0, 1, 2, 4))
        att_lo_ready = per_round("att_lo_ready", (0, 1, 2, 4))
        prod_done = per_round("prod_done", (0, 1, 3, 4))
        prod3b_done = sem("prod3b_done")
        val_ready = per_round("val_ready", (4,))
        val_hi_ready = per_round("val_hi_ready", (0, 1, 2, 4))
        val_lo_ready = per_round("val_lo_ready", (0, 1, 2, 4))
        val3_ready = [sem("val3a_ready"), sem("val3b_ready")]
        mix_done = per_round("mix_done")
        neg_ready = per_round("neg_ready", range(3))
        elu_exp_ready = per_round("elu_exp_ready", (1, 2))
        resid_ready = per_round("resid_ready", range(3))
        x_ready = per_round("x_ready", (0, 1, 2, 4))
        mix3_done = [mix_done[3], sem("mix3b_done")]
        neg3_ready = [sem("neg3a_ready"), sem("neg3b_ready")]
        exp3_ready = [sem("exp3a_ready"), sem("exp3b_ready")]
        sum3_ready = [sem("sum3a_ready"), sem("sum3b_ready")]
        h4_hi_ready = [sem("h4_hi_a_ready"), sem("h4_hi_b_ready")]
        h4_lo_ready = [sem("h4_lo_a_ready"), sem("h4_lo_b_ready")]
        rows_cleared, wait_passed = sem("rows_cleared"), sem("wait_passed")

        block = ctx.enter_context(nc.Block())

        @block.sync
        def _(sp):
            def turn(g0, g1, g2, g3, g4, g5, g6):
                if g0:
                    if g0.has_past(2):
                        sp.wait_ge(resid_ready[0], g0.count(back=2))
                    sp.dma_start(x_in[:, g0.slot, :], g0.row(x)).then_inc(x_loaded[g0.slot], 16)
                    if g0.has_past(2):
                        sp.wait_ge(masks_ready, g0.count(back=2))
                    sp.dma_start(adj_i[:, g0.slot, :], g0.row(adj)).then_inc(adj_loaded[g0.slot], 16)
                if g6:
                    sp.wait_ge(x_ready[4], g6.count())
                    sp.dma_start(g6.row(out), x_out[:, g6.slot, :]).then_inc(out_stored[g6.slot], 16)

            in_turns(sp, B, turn)
            for slot in range(2):
                sp.wait_ge(out_stored[slot], 16 * len(range(slot, B, 2)))

        @block.tensor
        def _(pe):
            def score_rows(r, hi, lo):
                for c in range(CH[r]):
                    for part in (hi, lo):
                        mm = pe.matmul(serial[CHAIN[r]][0:2 * NV[r], 0:P], v_r[r][:, c, :], part[:, c * P:(c + 1) * P],
                                       start=(c == 0 and part is hi), stop=(c == CH[r] - 1 and part is lo))
                return mm

            def product(r, hi, lo, c, q=0):
                a, b = hi[:, c * P:(c + 1) * P], lo[:, c * P:(c + 1) * P]
                wh, wl = w_hi[r][:, c, q * F:(q + 1) * F], w_lo[r][:, c, q * F:(q + 1) * F]
                dst = (mixed3[q] if r == 3 else mixed[r])[:]
                pe.matmul(dst, a, wh, start=(c == 0), stop=False)
                pe.matmul(dst, a, wl, start=False, stop=False)
                return pe.matmul(dst, b, wh, start=False, stop=(c == CH[r] - 1))

            def scores(k, heads, first):
                pe.matmul(serial[k][:, 0:heads * P], rows_r[k][:], sel_r[:, first + heads:first + 2 * heads, :],
                          start=True, stop=False)
                for h in range(heads):
                    mm = pe.matmul(serial[k][:, h * P:(h + 1) * P], sel_r[:, first + h, :], rows_r[k][:],
                                   start=False, stop=(h == heads - 1))
                return mm

            def mix(dst, k, h):
                pe.matmul(dst, att_hi[k][:, h, :], val_hi[k][:], start=True, stop=False)
                pe.matmul(dst, att_hi[k][:, h, :], val_lo[k][:], start=False, stop=False)
                return pe.matmul(dst, att_lo[k][:, h, :], val_hi[k][:], start=False, stop=True)

            def turn(g0, g1, g2, g3, g4, g5, g6):
                if g6:
                    for c in range(1, 6):
                        mm = product(4, h4_hi[:, g6.slot], h4_lo[:, g6.slot], c)
                if g6:
                    pe.wait_ge(rows_lo_ready[4], g6.count())
                    scores(3, 1, 0).then_inc(z_done[4], 1)
                if g5:
                    pe.wait_ge(xn_ready[3], g5.count())
                    for c in range(C):
                        mm = pe.transpose(serial[2][:, c * P:(c + 1) * P], xn[3][:, c * P:(c + 1) * P], eye[:])
                    mm.then_inc(hT_turned[3], 1)
                if g3:
                    pe.wait_ge(att_lo_ready[0], g3.count())
                    pe.wait_ge(val_lo_ready[0], g3.count())
                    mix(mixed[0][:], 0, 0).then_inc(mix_done[0], 1)
                if g6:
                    for c in range(6, 8):
                        mm = product(4, h4_hi[:, g6.slot], h4_lo[:, g6.slot], c)
                    mm.then_inc(prod_done[4], 1)
                if g5:
                    pe.wait_ge(lo_ready[3], g5.count())
                    score_rows(3, hT_hi[2], hT_lo[2]).then_inc(rows_done[3], 1)
                if g5:
                    product(3, hT_hi[2], hT_lo[2], 0, q=0)
                if g4:
                    pe.wait_ge(h_nat_ready, g4.count())
                    for c in range(C):
                        mm = pe.transpose(serial[1][:, c * P:(c + 1) * P], h_nat[:, c * P:(c + 1) * P], eye[:])
                    mm.then_inc(hT_turned[2], 1)
                if g5:
                    product(3, hT_hi[2], hT_lo[2], 1, q=0)
                if g5:
                    pe.wait_ge(rows_lo_ready[3], g5.count())
                    scores(2, H, 2).then_inc(z_done[3], 1)
                if g5:
                    for c in range(2, 4):
                        mm = product(3, hT_hi[2], hT_lo[2], c, q=0)
                    mm.then_inc(prod_done[3], 1)
                if g6:
                    pe.wait_ge(norm_done[4], g6.count())
                    pe.transpose(serial[3][:, 0:P], sc[3][:, 0, :], eye[:]).then_inc(att_turned[4], 1)
                if g4:
                    pe.wait_ge(lo_ready[2], g4.count())
                    score_rows(2, hT_hi[1], hT_lo[1]).then_inc(rows_done[2], 1)
                if g5:
                    product(3, hT_hi[2], hT_lo[2], 0, q=1)
                if g3:
                    pe.wait_ge(xn_ready[1], g3.count())
                    for c in range(C):
                        mm = pe.transpose(serial[0][:, c * P:(c + 1) * P], xn[1][:, c * P:(c + 1) * P], eye[:])
                    mm.then_inc(hT_turned[1], 1)
                if g5:
                    for c in range(1, 4):
                        mm = product(3, hT_hi[2], hT_lo[2], c, q=1)
                    mm.then_inc(prod3b_done, 1)
                if g4:
                    pe.wait_ge(rows_lo_ready[2], g4.count())
                    scores(1, 1, 0).then_inc(z_done[2], 1)
                if g3:
                    pe.wait_ge(lo_ready[1], g3.count())
                    score_rows(1, hT_hi[0], hT_lo[0]).then_inc(rows_done[1], 1)
                if g3:
                    for c in range(0, 2):
                        mm = product(1, hT_hi[0], hT_lo[0], c)
                if g3:
                    pe.wait_ge(rows_lo_ready[1], g3.count())
                    scores(0, 1, 0).then_inc(z_done[1], 1)
                if g5:
                    pe.wait_ge(norm_done[3], g5.count())
                    for h in range(H):
                        mm = pe.transpose(serial[2][:, h * P:(h + 1) * P], sc[2][:, h, :], eye[:])
                    mm.then_inc(att_turned[3], 1)
                if g3:
                    for c in range(2, 4):
                        mm = product(1, hT_hi[0], hT_lo[0], c)
                    mm.then_inc(prod_done[1], 1)
                if g5:
                    pe.wait_ge(att_ready[3], g5.count())
                    for f in range(C):
                        mm = pe.matmul(mixed3[0][:, f % C * P:(f % C + 1) * P], val3[:, f * P:(f + 1) * P],
                                       att3[:, f * P // FH, :], start=True, stop=True)
                    mm.then_inc(mix3_done[0], 1)
                if g3:
                    pe.wait_ge(norm_done[1], g3.count())
                    pe.transpose(serial[0][:, 0:P], sc[0][:, 0, :], eye[:]).then_inc(att_turned[1], 1)
                if g4:
                    pe.wait_ge(norm_done[2], g4.count())
                    pe.transpose(serial[1][:, 0:P], sc[1][:, 0, :], eye[:]).then_inc(att_turned[2], 1)
                if g5:
                    pe.wait_ge(val3_ready[1], g5.count())
                    for f in range(C, 2 * C):
                        mm = pe.matmul(mixed3[1][:, f % C * P:(f % C + 1) * P], val3[:, f * P:(f + 1) * P],
                                       att3[:, f * P // FH, :], start=True, stop=True)
                    mm.then_inc(mix3_done[1], 1)
                if g2:
                    pe.wait_ge(masks_ready, g2.count())
                    if g2.has_past(1):
                        pe.wait_ge(att_lo_ready[1], g2.count(back=1))
                    pe.transpose(serial[0][:, 0:P], m_le0[:], eye[:]).then_inc(m_le0_turned, 1)
                if g2:
                    pe.wait_ge(m_t_ready, g2.count())
                    for c in range(C):
                        mm = pe.transpose(serial[0][:, c * P:(c + 1) * P], xn[0][:, c * P:(c + 1) * P], eye[:])
                    mm.then_inc(hT_turned[0], 1)
                if g3:
                    pe.wait_ge(att_lo_ready[1], g3.count())
                    pe.wait_ge(val_lo_ready[1], g3.count())
                    mix(mixed[1][:], 0, 0).then_inc(mix_done[1], 1)
                if g4:
                    pe.wait_ge(att_lo_ready[2], g4.count())
                    pe.wait_ge(val_lo_ready[2], g4.count())
                    mix(mixed[2][:], 1, 0).then_inc(mix_done[2], 1)
                if g6:
                    pe.wait_ge(att_lo_ready[4], g6.count())
                    pe.wait_ge(val_lo_ready[4], g6.count())
                    mix(mixed[4][:], 3, 0).then_inc(mix_done[4], 1)
                if g2:
                    pe.wait_ge(lo_ready[0], g2.count())
                    score_rows(0, hT_hi[0], hT_lo[0]).then_inc(rows_done[0], 1)
                if g2:
                    for c in range(0, 4):
                        mm = product(0, hT_hi[0], hT_lo[0], c)
                    mm.then_inc(prod_done[0], 1)
                if g2:
                    pe.wait_ge(rows_lo_ready[0], g2.count())
                    scores(0, 1, 0).then_inc(z_done[0], 1)
                if g5:
                    pe.wait_ge(h4_lo_ready[1], g5.count())
                    if g5.has_next(2):
                        pe.wait_ge(x_ready[1], g5.count(back=-2))
                    score_rows(4, h4_hi[:, g5.slot], h4_lo[:, g5.slot]).then_inc(rows_done[4], 1)
                if g5:
                    if g5.has_past(1):
                        pe.wait_ge(x_ready[4], g5.count(back=1))
                    product(4, h4_hi[:, g5.slot], h4_lo[:, g5.slot], 0)

            pe.wait_ge(rows_cleared, 4)
            in_turns(pe, B, turn)

        @block.scalar
        def _(act):
            def exp_rows(k, h):
                return act.activation(sc[k][:, h, :], sc[k][:, h, :], ACT.Exp, scale=-1.0,
                                      bias=mn[k][:, h:h + 1], accum_out=sm[k][:, h:h + 1])

            def turn(g0, g1, g2, g3, g4, g5, g6):
                if g3:
                    if g3.has_past(1):
                        act.wait_ge(x_ready[1], g3.count(back=1))
                    act.activation(val0_f[:], mixed[0][:], ACT.Copy)
                    act.activation(val_hi[0][:], mixed[0][:], ACT.Copy).then_inc(val_hi_ready[0], 1)
                if g6:
                    act.wait_ge(rows_done[4], g6.count())
                    act.activation(rows_r[3][0:2 * NV[4], :], serial[3][0:2 * NV[4], 0:P], ACT.Copy).then_inc(rows_hi_ready[4], 1)
                if g3:
                    act.wait_ge(max_done[0], g3.count())
                    exp_rows(0, 0).then_inc(exp_done[0], 1)
                if g5:
                    act.wait_ge(rstd_ready[3], g5.count())
                    act.activation(xn[3][:], x_mid[2][:, g5.slot, :], ACT.Relu, scale=rstd[3][:], bias=nm[3][:]).then_inc(xn_ready[3], 1)
                if g6:
                    act.wait_ge(z_done[4], g6.count())
                    act.activation(sc[3][:].rearrange("p h n -> p (h n)"), serial[3][:, 0:P], ACT.Copy).then_inc(z_copied[4], 1)
                if g5:
                    act.wait_ge(hT_turned[3], g5.count())
                    act.activation(hT_hi[2][:], serial[2][:], ACT.Copy).then_inc(hi_ready[3], 1)
                if g3:
                    act.wait_ge(mix_done[0], g3.count())
                    act.activation(tmp[0][:, 0, :], mixed[0][:], ACT.Relu, scale=-SLOPE).then_inc(neg_ready[0], 1)
                if g4:
                    act.wait_ge(rstd_ready[2], g4.count())
                    act.activation(h_nat[:], x_mid[1][:, g4.slot, :], ACT.Relu, scale=rstd[2][:], bias=nm[2][:]).then_inc(h_nat_ready, 1)
                if g4:
                    act.wait_ge(h_nat_ready, g4.count())
                    act.activation(val_hi[1][:], h_nat[:], ACT.Copy).then_inc(val_hi_ready[2], 1)
                if g5:
                    act.wait_ge(rows_done[3], g5.count())
                    act.activation(rows_r[2][0:2 * NV[3], :], serial[2][0:2 * NV[3], 0:P], ACT.Copy).then_inc(rows_hi_ready[3], 1)
                if g6:
                    act.wait_ge(max_done[4], g6.count())
                    exp_rows(3, 0).then_inc(exp_done[4], 1)
                if g4:
                    act.wait_ge(hT_turned[2], g4.count())
                    act.activation(hT_hi[1][:], serial[1][:], ACT.Copy).then_inc(hi_ready[2], 1)
                if g6:
                    act.wait_ge(val_ready[4], g6.count())
                    act.activation(val_hi[3][:], x_out[:, g6.slot, :], ACT.Copy).then_inc(val_hi_ready[4], 1)
                if g5:
                    act.wait_ge(z_done[3], g5.count())
                    act.activation(sc[2][:].rearrange("p h n -> p (h n)"), serial[2][:, 0:H * P], ACT.Copy).then_inc(z_copied[3], 1)
                if g2:
                    act.wait_ge(rstd_ready[0], g2.count())
                    act.activation(xn[0][:], x_in[:, g2.slot, :], ACT.Relu, scale=rstd[0][:], bias=nm[0][:]).then_inc(xn_ready[0], 1)
                if g3:
                    act.wait_ge(rstd_ready[1], g3.count())
                    act.activation(xn[1][:], x_mid[0][:, g3.slot, :], ACT.Relu, scale=rstd[1][:], bias=nm[1][:]).then_inc(xn_ready[1], 1)
                if g6:
                    act.wait_ge(att_turned[4], g6.count())
                    act.activation(att_hi[3][:].rearrange("p h n -> p (h n)"), serial[3][:, 0:P], ACT.Copy).then_inc(att_hi_ready[4], 1)
                if g4:
                    act.wait_ge(rows_done[2], g4.count())
                    act.activation(rows_r[1][0:2 * NV[2], :], serial[1][0:2 * NV[2], 0:P], ACT.Copy).then_inc(rows_hi_ready[2], 1)
                if g3:
                    act.wait_ge(hT_turned[1], g3.count())
                    act.activation(hT_hi[0][:], serial[0][:], ACT.Copy).then_inc(hi_ready[1], 1)
                if g5:
                    act.wait_ge(max_done[3], g5.count())
                    for h in range(H):
                        ins = exp_rows(2, h)
                    ins.then_inc(exp_done[3], 1)
                if g4:
                    act.wait_ge(z_done[2], g4.count())
                    act.activation(sc[1][:].rearrange("p h n -> p (h n)"), serial[1][:, 0:P], ACT.Copy).then_inc(z_copied[2], 1)
                if g3:
                    act.wait_ge(rows_done[1], g3.count())
                    act.activation(rows_r[0][0:2 * NV[1], :], serial[0][0:2 * NV[1], 0:P], ACT.Copy).then_inc(rows_hi_ready[1], 1)
                if g4:
                    act.wait_ge(max_done[2], g4.count())
                    exp_rows(1, 0).then_inc(exp_done[2], 1)
                if g3:
                    act.wait_ge(z_done[1], g3.count())
                    act.activation(sc[0][:].rearrange("p h n -> p (h n)"), serial[0][:, 0:P], ACT.Copy).then_inc(z_copied[1], 1)
                if g5:
                    act.wait_ge(att_turned[3], g5.count())
                    act.activation(att3[:].rearrange("p h n -> p (h n)"), serial[2][:, 0:H * P], ACT.Copy).then_inc(att_ready[3], 1)
                if g3:
                    act.wait_ge(max_done[1], g3.count())
                    exp_rows(0, 0).then_inc(exp_done[1], 1)
                if g3:
                    act.wait_ge(prod_done[1], g3.count())
                    act.activation(val0_f[:], mixed[1][:], ACT.Copy)
                    act.activation(val_hi[0][:], mixed[1][:], ACT.Copy).then_inc(val_hi_ready[1], 1)
                if g3:
                    act.wait_ge(att_turned[1], g3.count())
                    act.activation(att_hi[0][:].rearrange("p h n -> p (h n)"), serial[0][:, 0:P], ACT.Copy).then_inc(att_hi_ready[1], 1)
                if g5:
                    act.wait_ge(mix3_done[0], g5.count())
                    act.activation(tmp[2][:, 0, :], mixed3[0][:], ACT.Relu, scale=-1.0).then_inc(neg3_ready[0], 1)
                if g4:
                    act.wait_ge(att_turned[2], g4.count())
                    act.activation(att_hi[1][:].rearrange("p h n -> p (h n)"), serial[1][:, 0:P], ACT.Copy).then_inc(att_hi_ready[2], 1)
                if g2:
                    act.wait_ge(m_le0_turned, g2.count())
                    if g2.has_past(2):
                        act.wait_ge(m_self_ready, g2.count(back=2))
                    act.activation(m_t[:, g2.slot, :], serial[0][:, 0:P], ACT.Copy).then_inc(m_t_ready, 1)
                if g5:
                    act.wait_ge(neg3_ready[0], g5.count())
                    act.activation(tmp[2][:, 0, :], tmp[2][:, 0, :], ACT.Exp, scale=-1.0).then_inc(exp3_ready[0], 1)
                if g5:
                    act.wait_ge(mix3_done[1], g5.count())
                    act.activation(tmp[2][:, 1, :], mixed3[1][:], ACT.Relu, scale=-1.0).then_inc(neg3_ready[1], 1)
                if g2:
                    act.wait_ge(hT_turned[0], g2.count())
                    act.activation(hT_hi[0][:], serial[0][:], ACT.Copy).then_inc(hi_ready[0], 1)
                if g5:
                    act.wait_ge(neg3_ready[1], g5.count())
                    act.activation(tmp[2][:, 1, :], tmp[2][:, 1, :], ACT.Exp, scale=-1.0).then_inc(exp3_ready[1], 1)
                if g3:
                    act.wait_ge(mix_done[1], g3.count())
                    act.activation(tmp[0][:, 0, :], mixed[1][:], ACT.Relu, scale=-1.0).then_inc(neg_ready[1], 1)
                if g5:
                    act.wait_ge(sum3_ready[0], g5.count())
                    act.activation(h4_hi[:, g5.slot, 0:F], tmp[2][:, 0, :], ACT.Copy, bias=-1.0).then_inc(h4_hi_ready[0], 1)
                if g3:
                    act.wait_ge(neg_ready[1], g3.count())
                    act.activation(tmp[0][:, 0, :], tmp[0][:, 0, :], ACT.Exp, scale=-1.0).then_inc(elu_exp_ready[1], 1)
                if g5:
                    act.wait_ge(sum3_ready[1], g5.count())
                    act.activation(h4_hi[:, g5.slot, F:2 * F], tmp[2][:, 1, :], ACT.Copy, bias=-1.0).then_inc(h4_hi_ready[1], 1)
                if g4:
                    act.wait_ge(mix_done[2], g4.count())
                    act.activation(tmp[1][:, 0, :], mixed[2][:], ACT.Relu, scale=-1.0).then_inc(neg_ready[2], 1)
                if g2:
                    act.wait_ge(rows_done[0], g2.count())
                    act.activation(rows_r[0][0:2 * NV[0], :], serial[0][0:2 * NV[0], 0:P], ACT.Copy).then_inc(rows_hi_ready[0], 1)
                if g4:
                    act.wait_ge(neg_ready[2], g4.count())
                    act.activation(tmp[1][:, 0, :], tmp[1][:, 0, :], ACT.Exp, scale=-1.0).then_inc(elu_exp_ready[2], 1)
                if g2:
                    act.wait_ge(z_done[0], g2.count())
                    act.activation(sc[0][:].rearrange("p h n -> p (h n)"), serial[0][:, 0:P], ACT.Copy).then_inc(z_copied[0], 1)

            in_turns(act, B, turn)

        @block.gpsimd
        def _(pool):
            def turn(g0, g1, g2, g3, g4, g5, g6):
                if g3:
                    pool.wait_ge(val_hi_ready[0], g3.count())
                    pool.tensor_tensor(val_lo[0][:], val0_f[:], val_hi[0][:].bitcast(F32), ALU.subtract).then_inc(val_lo_ready[0], 1)
                if g4:
                    pool.wait_ge(moments_ready[2], g4.count())
                    pool.tensor_tensor(ve[2][:], mv[2][:, 1:2], eps[:], ALU.add)
                    pool.tensor_tensor(nm[2][:], zero[:], mv[2][:, 0:1], ALU.subtract).then_inc(vareps_ready[2], 1)
                    pool.wait_ge(vareps_ready[2], g4.count())
                    pool.tensor_tensor(rstd[2][:], ve[2][:], half[:], ALU.pow).then_inc(rstd_done[2], 1)
                    pool.wait_ge(rstd_done[2], g4.count())
                    pool.tensor_tensor(nm[2][:], nm[2][:], rstd[2][:], ALU.mult).then_inc(rstd_ready[2], 1)
                if g3:
                    pool.wait_ge(neg_ready[0], g3.count())
                    pool.tensor_tensor(tmp[0][:, 0, :], x_in[:, g3.slot, :], tmp[0][:, 0, :], ALU.subtract).then_inc(resid_ready[0], 1)
                if g2:
                    pool.wait_ge(moments_ready[0], g2.count())
                    pool.tensor_tensor(ve[0][:], mv[0][:, 1:2], eps[:], ALU.add)
                    pool.tensor_tensor(nm[0][:], zero[:], mv[0][:, 0:1], ALU.subtract).then_inc(vareps_ready[0], 1)
                    pool.wait_ge(vareps_ready[0], g2.count())
                    pool.tensor_tensor(rstd[0][:], ve[0][:], half[:], ALU.pow).then_inc(rstd_done[0], 1)
                    pool.wait_ge(rstd_done[0], g2.count())
                    pool.tensor_tensor(nm[0][:], nm[0][:], rstd[0][:], ALU.mult).then_inc(rstd_ready[0], 1)
                if g3:
                    pool.wait_ge(moments_ready[1], g3.count())
                    pool.tensor_tensor(ve[1][:], mv[1][:, 1:2], eps[:], ALU.add)
                    pool.tensor_tensor(nm[1][:], zero[:], mv[1][:, 0:1], ALU.subtract).then_inc(vareps_ready[1], 1)
                    pool.wait_ge(vareps_ready[1], g3.count())
                    pool.tensor_tensor(rstd[1][:], ve[1][:], half[:], ALU.pow).then_inc(rstd_done[1], 1)
                    pool.wait_ge(rstd_done[1], g3.count())
                    pool.tensor_tensor(nm[1][:], nm[1][:], rstd[1][:], ALU.mult).then_inc(rstd_ready[1], 1)
                if g4:
                    if g4.has_past(2):
                        pool.wait_ge(max_done[4], g4.count(back=2))
                    pool.tensor_tensor(m_self[:, g4.slot, :], m_t[:, g4.slot, :], noteye[:], ALU.mult).then_inc(m_self_ready, 1)
                if g5:
                    pool.wait_ge(recip_done[3], g5.count())
                    pool.tensor_tensor(sc[2][:], sc[2][:], rc[2][:].rearrange("p (h o) -> p h o", o=1).broadcast_to([P, H, P]),
                                       ALU.mult).then_inc(norm_done[3], 1)
                if g4:
                    pool.wait_ge(val_hi_ready[2], g4.count())
                    pool.wait_ge(hT_turned[2], g4.count())
                    pool.tensor_tensor(val_lo[1][:], h_nat[:], val_hi[1][:].bitcast(F32), ALU.subtract).then_inc(val_lo_ready[2], 1)
                if g6:
                    pool.wait_ge(val_hi_ready[4], g6.count())
                    pool.tensor_tensor(val_lo[3][:], x_out[:, g6.slot, :], val_hi[3][:].bitcast(F32), ALU.subtract).then_inc(val_lo_ready[4], 1)
                if g3:
                    pool.wait_ge(val_hi_ready[1], g3.count())
                    pool.tensor_tensor(val_lo[0][:], val0_f[:], val_hi[0][:].bitcast(F32), ALU.subtract).then_inc(val_lo_ready[1], 1)
                if g3:
                    pool.wait_ge(elu_exp_ready[1], g3.count())
                    pool.tensor_tensor(tmp[0][:, 0, :], x_mid[0][:, g3.slot, :], tmp[0][:, 0, :], ALU.add).then_inc(resid_ready[1], 1)
                if g4:
                    pool.wait_ge(elu_exp_ready[2], g4.count())
                    pool.tensor_tensor(tmp[1][:, 0, :], x_mid[1][:, g4.slot, :], tmp[1][:, 0, :], ALU.add).then_inc(resid_ready[2], 1)
                if g4:
                    pool.wait_ge(moments_ready[3], g4.count())
                    pool.tensor_tensor(ve[3][:], mv[3][:, 1:2], eps[:], ALU.add)
                    pool.tensor_tensor(nm[3][:], zero[:], mv[3][:, 0:1], ALU.subtract).then_inc(vareps_ready[3], 1)
                    pool.wait_ge(vareps_ready[3], g4.count())
                    pool.tensor_tensor(rstd[3][:], ve[3][:], half[:], ALU.pow).then_inc(rstd_done[3], 1)
                    pool.wait_ge(rstd_done[3], g4.count())
                    pool.tensor_tensor(nm[3][:], nm[3][:], rstd[3][:], ALU.mult).then_inc(rstd_ready[3], 1)

            in_turns(pool, B, turn)

        @block.vector
        def _(dve):
            def masked_min(k, h, mask):
                return dve.tensor_tensor_reduce(sc[k][:, h, :], sc[k][:, h, :], mask, 1.0, 3.0e38,
                                                ALU.add, ALU.min, mn[k][:, h:h + 1])

            def turn(g0, g1, g2, g3, g4, g5, g6):
                if g6:
                    dve.wait_ge(rows_hi_ready[4], g6.count())
                    dve.tensor_tensor(rows_r[3][LOROW:LOROW + 2 * NV[4], :], serial[3][0:2 * NV[4], 0:P], rows_r[3][0:2 * NV[4], :].bitcast(F32),
                                      ALU.subtract).then_inc(rows_lo_ready[4], 1)
                if g3:
                    dve.wait_ge(leaky_done[0], g3.count())
                    dve.sem_inc(wait_passed, 1)
                    masked_min(0, 0, m_t[:, g3.slot, :]).then_inc(max_done[0], 1)
                if g4:
                    dve.bn_stats(st[2][:], x_mid[1][:, g4.slot, :]).then_inc(stats_done[2], 1)
                if g3:
                    dve.wait_ge(exp_done[0], g3.count())
                    dve.reciprocal(rc[0][:], sm[0][:]).then_inc(recip_done[0], 1)
                if g3:
                    dve.wait_ge(recip_done[0], g3.count())
                    dve.tensor_scalar(att_hi[0][:, 0, :], sc[0][:, 0, :], rc[0][:], None, ALU.mult).then_inc(att_hi_ready[0], 1)
                if g3:
                    dve.wait_ge(att_hi_ready[0], g3.count())
                    dve.scalar_tensor_tensor(out=att_lo[0][:, 0, :], in0=sc[0][:, 0, :], scalar=rc[0][:], in1=att_hi[0][:, 0, :].bitcast(F32),
                                             op0=ALU.mult, op1=ALU.subtract).then_inc(att_lo_ready[0], 1)
                if g4:
                    dve.wait_ge(stats_done[2], g4.count())
                    dve.sem_inc(wait_passed, 1)
                    dve.bn_aggr(mv[2][:], st[2][:]).then_inc(moments_ready[2], 1)
                if g6:
                    dve.wait_ge(z_copied[4], g6.count())
                    dve.scalar_tensor_tensor(out=sc[3][:], in0=sc[3][:], scalar=SLOPE, in1=sc[3][:],
                                             op0=ALU.mult, op1=ALU.min).then_inc(leaky_done[4], 1)
                if g6:
                    dve.wait_ge(leaky_done[4], g6.count())
                    dve.sem_inc(wait_passed, 1)
                    masked_min(3, 0, m_self[:, g6.slot, :]).then_inc(max_done[4], 1)
                if g2:
                    dve.wait_ge(stats_done[0], g2.count())
                    dve.sem_inc(wait_passed, 1)
                    dve.bn_aggr(mv[0][:], st[0][:]).then_inc(moments_ready[0], 1)
                if g5:
                    dve.wait_ge(hi_ready[3], g5.count())
                    dve.tensor_tensor(hT_lo[2][:], serial[2][:], hT_hi[2][:].bitcast(F32), ALU.subtract).then_inc(lo_ready[3], 1)
                if g6:
                    dve.wait_ge(prod_done[4], g6.count())
                    if g6.has_past(2):
                        dve.wait_ge(out_stored[g6.slot], g6.dma_count(back=2))
                    dve.tensor_tensor(x_out[:, g6.slot, :], mixed[4][:], bias4[:], ALU.add).then_inc(val_ready[4], 1)
                if g3:
                    dve.wait_ge(resid_ready[0], g3.count())
                    dve.scalar_tensor_tensor(out=x_mid[0][:, g3.slot, :], in0=mixed[0][:], scalar=0.0, in1=tmp[0][:, 0, :],
                                             op0=ALU.max, op1=ALU.add).then_inc(x_ready[0], 1)
                if g5:
                    dve.wait_ge(rows_hi_ready[3], g5.count())
                    dve.tensor_tensor(rows_r[2][LOROW:LOROW + 2 * NV[3], :], serial[2][0:2 * NV[3], 0:P], rows_r[2][0:2 * NV[3], :].bitcast(F32),
                                      ALU.subtract).then_inc(rows_lo_ready[3], 1)
                if g6:
                    dve.wait_ge(exp_done[4], g6.count())
                    dve.reciprocal(rc[3][:], sm[3][:]).then_inc(recip_done[4], 1)
                if g3:
                    dve.wait_ge(x_ready[0], g3.count())
                    dve.bn_stats(st[1][:], x_mid[0][:, g3.slot, :]).then_inc(stats_done[1], 1)
                if g3:
                    dve.wait_ge(stats_done[1], g3.count())
                    dve.sem_inc(wait_passed, 1)
                    dve.bn_aggr(mv[1][:], st[1][:]).then_inc(moments_ready[1], 1)
                if g6:
                    dve.wait_ge(recip_done[4], g6.count())
                    dve.tensor_scalar(sc[3][:, 0, :], sc[3][:, 0, :], rc[3][:], None, ALU.mult).then_inc(norm_done[4], 1)
                if g4:
                    dve.wait_ge(hi_ready[2], g4.count())
                    dve.tensor_tensor(hT_lo[1][:], serial[1][:], hT_hi[1][:].bitcast(F32), ALU.subtract).then_inc(lo_ready[2], 1)
                if g5:
                    dve.wait_ge(z_copied[3], g5.count())
                    dve.scalar_tensor_tensor(out=sc[2][:], in0=sc[2][:], scalar=SLOPE, in1=sc[2][:],
                                             op0=ALU.mult, op1=ALU.min).then_inc(leaky_done[3], 1)
                if g5:
                    dve.wait_ge(leaky_done[3], g5.count())
                    dve.sem_inc(wait_passed, 1)
                    for h in range(H):
                        ins = masked_min(2, h, m_self[:, g5.slot, :])
                    ins.then_inc(max_done[3], 1)
                if g4:
                    dve.wait_ge(rows_hi_ready[2], g4.count())
                    dve.tensor_tensor(rows_r[1][LOROW:LOROW + 2 * NV[2], :], serial[1][0:2 * NV[2], 0:P], rows_r[1][0:2 * NV[2], :].bitcast(F32),
                                      ALU.subtract).then_inc(rows_lo_ready[2], 1)
                if g6:
                    dve.wait_ge(att_hi_ready[4], g6.count())
                    dve.tensor_tensor(att_lo[3][:].rearrange("p h n -> p (h n)"), serial[3][:, 0:P], att_hi[3][:].rearrange("p h n -> p (h n)").bitcast(F32),
                                      ALU.subtract).then_inc(att_lo_ready[4], 1)
                if g3:
                    dve.wait_ge(hi_ready[1], g3.count())
                    dve.tensor_tensor(hT_lo[0][:], serial[0][:], hT_hi[0][:].bitcast(F32), ALU.subtract).then_inc(lo_ready[1], 1)
                if g5:
                    dve.tensor_tensor(val3[:, 0:F], mixed3[0][:], bias3[:, 0:F], ALU.add).then_inc(val3_ready[0], 1)
                if g5:
                    dve.wait_ge(exp_done[3], g5.count())
                    dve.reciprocal(rc[2][:], sm[2][:]).then_inc(recip_done[3], 1)
                if g4:
                    dve.wait_ge(z_copied[2], g4.count())
                    dve.scalar_tensor_tensor(out=sc[1][:], in0=sc[1][:], scalar=SLOPE, in1=sc[1][:],
                                             op0=ALU.mult, op1=ALU.min).then_inc(leaky_done[2], 1)
                if g4:
                    dve.wait_ge(leaky_done[2], g4.count())
                    dve.sem_inc(wait_passed, 1)
                    masked_min(1, 0, m_nat[:, g4.slot, :]).then_inc(max_done[2], 1)
                if g3:
                    dve.wait_ge(rows_hi_ready[1], g3.count())
                    dve.tensor_tensor(rows_r[0][LOROW:LOROW + 2 * NV[1], :], serial[0][0:2 * NV[1], 0:P], rows_r[0][0:2 * NV[1], :].bitcast(F32),
                                      ALU.subtract).then_inc(rows_lo_ready[1], 1)
                if g5:
                    dve.wait_ge(prod3b_done, g5.count())
                    dve.tensor_tensor(val3[:, F:2 * F], mixed3[1][:], bias3[:, F:2 * F], ALU.add).then_inc(val3_ready[1], 1)
                if g3:
                    dve.wait_ge(z_copied[1], g3.count())
                    dve.scalar_tensor_tensor(out=sc[0][:], in0=sc[0][:], scalar=SLOPE, in1=sc[0][:],
                                             op0=ALU.mult, op1=ALU.min).then_inc(leaky_done[1], 1)
                if g3:
                    dve.wait_ge(leaky_done[1], g3.count())
                    dve.sem_inc(wait_passed, 1)
                    masked_min(0, 0, m_nat[:, g3.slot, :]).then_inc(max_done[1], 1)
                if g4:
                    dve.wait_ge(exp_done[2], g4.count())
                    dve.reciprocal(rc[1][:], sm[1][:]).then_inc(recip_done[2], 1)
                if g4:
                    dve.wait_ge(recip_done[2], g4.count())
                    dve.tensor_scalar(sc[1][:, 0, :], sc[1][:, 0, :], rc[1][:], None, ALU.mult).then_inc(norm_done[2], 1)
                if g3:
                    dve.wait_ge(exp_done[1], g3.count())
                    dve.reciprocal(rc[0][:], sm[0][:]).then_inc(recip_done[1], 1)
                if g3:
                    dve.wait_ge(recip_done[1], g3.count())
                    dve.tensor_scalar(sc[0][:, 0, :], sc[0][:, 0, :], rc[0][:], None, ALU.mult).then_inc(norm_done[1], 1)
                if g2:
                    dve.wait_ge(adj_loaded[g2.slot], g2.dma_count())
                    dve.tensor_scalar(m_nat[:, g2.slot, :], adj_i[:, g2.slot, :], 0, BIG, ALU.is_equal, ALU.mult)
                    dve.tensor_scalar(m_le0[:], adj_i[:, g2.slot, :], 0, BIG, ALU.is_le, ALU.mult).then_inc(masks_ready, 1)
                if g3:
                    dve.wait_ge(att_hi_ready[1], g3.count())
                    dve.tensor_tensor(att_lo[0][:].rearrange("p h n -> p (h n)"), serial[0][:, 0:P], att_hi[0][:].rearrange("p h n -> p (h n)").bitcast(F32),
                                      ALU.subtract).then_inc(att_lo_ready[1], 1)
                if g4:
                    dve.wait_ge(att_hi_ready[2], g4.count())
                    dve.tensor_tensor(att_lo[1][:].rearrange("p h n -> p (h n)"), serial[1][:, 0:P], att_hi[1][:].rearrange("p h n -> p (h n)").bitcast(F32),
                                      ALU.subtract).then_inc(att_lo_ready[2], 1)
                if g5:
                    dve.wait_ge(exp3_ready[0], g5.count())
                    dve.scalar_tensor_tensor(out=tmp[2][:, 0, :], in0=mixed3[0][:], scalar=0.0, in1=tmp[2][:, 0, :],
                                             op0=ALU.max, op1=ALU.add).then_inc(sum3_ready[0], 1)
                if g2:
                    dve.wait_ge(hi_ready[0], g2.count())
                    dve.tensor_tensor(hT_lo[0][:], serial[0][:], hT_hi[0][:].bitcast(F32), ALU.subtract).then_inc(lo_ready[0], 1)
                if g5:
                    dve.wait_ge(exp3_ready[1], g5.count())
                    dve.scalar_tensor_tensor(out=tmp[2][:, 1, :], in0=mixed3[1][:], scalar=0.0, in1=tmp[2][:, 1, :],
                                             op0=ALU.max, op1=ALU.add).then_inc(sum3_ready[1], 1)
                if g1:
                    dve.wait_ge(x_loaded[g1.slot], g1.dma_count())
                    dve.bn_stats(st[0][:], x_in[:, g1.slot, :]).then_inc(stats_done[0], 1)
                if g5:
                    dve.wait_ge(h4_hi_ready[0], g5.count())
                    dve.scalar_tensor_tensor(out=h4_lo[:, g5.slot, 0:F], in0=tmp[2][:, 0, :], scalar=-1.0,
                                             in1=h4_hi[:, g5.slot, 0:F].bitcast(F32),
                                             op0=ALU.add, op1=ALU.subtract).then_inc(h4_lo_ready[0], 1)
                if g5:
                    dve.wait_ge(h4_hi_ready[1], g5.count())
                    dve.scalar_tensor_tensor(out=h4_lo[:, g5.slot, F:2 * F], in0=tmp[2][:, 1, :], scalar=-1.0,
                                             in1=h4_hi[:, g5.slot, F:2 * F].bitcast(F32),
                                             op0=ALU.add, op1=ALU.subtract).then_inc(h4_lo_ready[1], 1)
                if g2:
                    dve.wait_ge(rows_hi_ready[0], g2.count())
                    dve.tensor_tensor(rows_r[0][LOROW:LOROW + 2 * NV[0], :], serial[0][0:2 * NV[0], 0:P], rows_r[0][0:2 * NV[0], :].bitcast(F32),
                                      ALU.subtract).then_inc(rows_lo_ready[0], 1)
                if g3:
                    dve.wait_ge(resid_ready[1], g3.count())
                    dve.scalar_tensor_tensor(out=x_mid[1][:, g3.slot, :], in0=mixed[1][:], scalar=0.0, in1=tmp[0][:, 0, :],
                                             op0=ALU.max, op1=ALU.add).then_inc(x_ready[1], 1)
                if g6:
                    dve.wait_ge(mix_done[4], g6.count())
                    dve.tensor_tensor(x_out[:, g6.slot, :], mixed[4][:], x_mid[2][:, g6.slot, :], ALU.add).then_inc(x_ready[4], 1)
                if g4:
                    dve.wait_ge(resid_ready[2], g4.count())
                    if g4.has_past(2):
                        dve.wait_ge(x_ready[4], g4.count(back=2))
                    dve.scalar_tensor_tensor(out=x_mid[2][:, g4.slot, :], in0=mixed[2][:], scalar=0.0, in1=tmp[1][:, 0, :],
                                             op0=ALU.max, op1=ALU.add).then_inc(x_ready[2], 1)
                if g4:
                    dve.wait_ge(x_ready[2], g4.count())
                    dve.bn_stats(st[3][:], x_mid[2][:, g4.slot, :]).then_inc(stats_done[3], 1)
                if g4:
                    dve.wait_ge(stats_done[3], g4.count())
                    dve.sem_inc(wait_passed, 1)
                    dve.bn_aggr(mv[3][:], st[3][:]).then_inc(moments_ready[3], 1)
                if g2:
                    dve.wait_ge(z_copied[0], g2.count())
                    dve.scalar_tensor_tensor(out=sc[0][:], in0=sc[0][:], scalar=SLOPE, in1=sc[0][:],
                                             op0=ALU.mult, op1=ALU.min).then_inc(leaky_done[0], 1)

            for k in range(4):
                dve.memset(rows_r[k][:].bitcast(F32), 0.0).then_inc(rows_cleared, 1)
            dve.wait_ge(rows_cleared, 4)
            in_turns(dve, B, turn)


def kernel(x, adj, L0_gnn_W, L0_gnn_a, L1_gnn_W, L1_gnn_a, L2_gnn_W_fc, L2_gnn_W_attn, L3_gnn_W1,
           L3_gnn_att_src1, L3_gnn_att_dst1, L3_gnn_b1, L3_gnn_W2, L3_gnn_att_src2, L3_gnn_att_dst2,
           L3_gnn_b2):
    import numpy as np
    import concourse.bacc as bacc
    from concourse.bass_utils import run_bass_kernel_spmd

    heads = L3_gnn_att_src1.shape[0]
    sel = np.zeros((KSEL, 2 + 2 * heads, P), np.float32)
    for part in (0, LOROW):
        for vec in range(2):
            for hl in range(2):
                sel[part + 2 * hl + vec, vec] = 1.0
                for h in range(heads):
                    sel[part + 2 * heads * hl + heads * vec + h, 2 + heads * vec + h] = 1.0
    named = dict(x=x, adj=adj, w0=L0_gnn_W, a0=L0_gnn_a, w1=L1_gnn_W, a1=L1_gnn_a, wfc=L2_gnn_W_fc,
                 afc=L2_gnn_W_attn, w3=L3_gnn_W1, as3=L3_gnn_att_src1, ad3=L3_gnn_att_dst1, b3=L3_gnn_b1,
                 w4=L3_gnn_W2, as4=L3_gnn_att_src2, ad4=L3_gnn_att_dst2, b4=L3_gnn_b2,
                 ident=np.eye(P, dtype=np.float32), sel=sel)
    nc = bacc.Bacc("TRN2", target_bir_lowering=False, num_devices=1)
    arrays, args = {}, {}
    for name, a in named.items():
        arrays[f"in_{name}"] = np.ascontiguousarray(a)
        args[name] = nc.dram_tensor(f"in_{name}", a.shape, mybir.dt.from_np(arrays[f"in_{name}"].dtype),
                                    kind="ExternalInput").ap()
    out = nc.dram_tensor("out", x.shape, F32, kind="ExternalOutput").ap()
    gat_layers_kernel(nc, out=out, **args)
    return run_bass_kernel_spmd(nc, [arrays], core_ids=[0]).results[0]["out"]
```

```python
from contextlib import ExitStack

import concourse.bass as bass
from concourse import mybir

ALU = mybir.AluOpType
ACT = mybir.ActivationFunctionType
F32 = mybir.dt.float32
F32R = mybir.dt.float32r
I32 = mybir.dt.int32

P = 128
KSEL = 64
LOROW = 32
BIG = 1.0e30
EPS = 1e-5
SLOPE = 0.2
ROUNDS = 5


OLDEST = 5


class Graph:

    def __init__(self, engine, base, offset, values, graphs):
        self.graphs = graphs
        self.engine, self.base, self.offset, self.values = engine, base, offset, values
        self.slot = offset % 2

    def has_past(self, back):
        return self.base is not None or self.offset >= back

    def has_next(self, ahead):
        return self.base is not None or self.offset + ahead < self.graphs

    def value(self, more, unit):
        if self.base is None:
            return unit * (self.offset + more)
        key = (self.offset + more, unit)
        if key not in self.values:
            self.values[key] = self.engine.snap((self.base + (self.offset + more)) * unit)
        return self.values[key]

    def count(self, back=0):
        return self.value(1 - back, 1)

    def dma_count(self, back=0):
        return self.value(2 - back - self.slot, 8)

    def row(self, tensor):
        return tensor[self.offset if self.base is None else self.base + self.offset]


def in_turns(engine, graphs, turn):
    head = OLDEST + 2 + OLDEST % 2
    passes = (graphs - head) // 2
    tail = head + 2 * passes if passes > 0 else head

    def peeled(t):
        turn(*(Graph(engine, None, t - n, None, graphs) if 0 <= t - n < graphs else None for n in range(OLDEST + 1)))

    for t in range(head):
        peeled(t)
    if passes > 0:
        with engine.Fori(head, tail - 1, 2) as t0:
            values = {}
            for u in range(2):
                turn(*(Graph(engine, t0, u - n, values, graphs) for n in range(OLDEST + 1)))
    for t in range(tail, graphs + OLDEST):
        peeled(t)


def prepare_weights(nc, consts, dram):
    (eye, noteye, half, eps, zero, sel_r, w_hi, w_lo, v_f, v_r, NV, bias3, bias4) = consts
    (w0, a0, w1, a1, wfc, afc, w3, as3, ad3, b3, w4, as4, ad4, b4, ident, sel) = dram
    H, FH = as3.shape
    F, HF = w3.shape
    O = wfc.shape[0]

    with ExitStack() as ctx:
        def sb(name, shape, dt=F32):
            return ctx.enter_context(nc.sbuf_tensor("setup_" + name, list(shape), dt))

        setup_sems = []

        def sem(name):
            setup_sems.append(nc.alloc_semaphore(name="setup_" + name))
            return setup_sems[-1]

        w_f = [sb(f"w{r}", w_hi[r].shape) if w_hi[r] is not None else None for r in range(ROUNDS)]
        wfc_f = sb("wfc", [O, F])
        afc_f = sb("afc", [O, 2])
        sel_f = sb("sel", [KSEL] + list(sel_r.shape)[1:])
        a_b = [sb(f"a{r}", [P, n]) if n else None for r, n in enumerate((2 * F, 2 * F, 0, 2 * HF, 2 * F))]
        junk = sb("junk", [P, 2, F])
        vfc = ctx.enter_context(nc.psum_tensor("setup_vfc", [P, F // P, 2], F32))

        consts_loaded, biases_loaded = sem("consts_loaded"), sem("biases_loaded")
        w_loaded = [sem(f"w{r}_loaded") for r in range(ROUNDS)]
        a_loaded = [sem(f"a{r}_loaded") for r in range(ROUNDS)]
        hi_ready, lo_ready = sem("hi_ready"), sem("lo_ready")
        dots_done, vfc_done, v_hi_ready = sem("dots_done"), sem("vfc_done"), sem("v_hi_ready")
        DOTS = [2 if r == 2 else v_f[r].shape[1] * NV[r] for r in range(ROUNDS)]
        SPLIT = [r for r in range(ROUNDS) if w_hi[r] is not None]

        with nc.Block() as block:

            @block.sync
            def _(sp):
                def row(v):
                    return v.rearrange("(o n) -> o n", o=1)

                def load(dst, src, signal):
                    sp.dma_start(dst, src).then_inc(signal, 16)

                w_dram = {0: w0, 1: w1, 3: w3, 4: w4}
                cols = {0: a0.rearrange("n x -> x n"), 1: a1.rearrange("n x -> x n")}
                for r in SPLIT:
                    if r in (0, 1):
                        load(a_b[r][:], cols[r].broadcast_to([P, 2 * F]), a_loaded[r])
                    else:
                        for k, a in enumerate((as3, ad3) if r == 3 else (as4, ad4)):
                            n = HF if r == 3 else F
                            load(a_b[r][:, k * n:(k + 1) * n], row(a.rearrange("h f -> (h f)")).broadcast_to([P, n]), a_loaded[r])
                    load(w_f[r][:], w_dram[r].rearrange("(c p) n -> p c n", p=P), w_loaded[r])
                    if r == 0:
                        load(wfc_f[:], wfc, consts_loaded)
                        with nc.allow_non_contiguous_dma(reason="64 floats, once"):
                            load(afc_f[:], afc.rearrange("x (k o) -> o (x k)", k=2), consts_loaded)
                        load(eye[:], ident, consts_loaded)
                        load(sel_f[:], sel, consts_loaded)
                load(bias3[:], row(b3).broadcast_to([P, HF]), biases_loaded)
                load(bias4[:], row(b4).broadcast_to([P, F]), biases_loaded)

            @block.scalar
            def _(act):
                for n, r in enumerate(SPLIT):
                    act.wait_ge(w_loaded[r], 16)
                    act.activation(w_hi[r][:], w_f[r][:], ACT.Copy).then_inc(hi_ready, 1)
                for r in range(ROUNDS):
                    act.wait_ge(dots_done, sum(DOTS[:r + 1]))
                    act.activation(v_r[r][:, :, 0:NV[r]], v_f[r][:], ACT.Copy).then_inc(v_hi_ready, 1)

            @block.gpsimd
            def _(pool):
                pool.memset(half[:], -0.5)
                pool.memset(eps[:], EPS)
                pool.memset(zero[:], 0.0)
                pool.wait_ge(consts_loaded, 4 * 16)
                pool.tensor_scalar(noteye[:], eye[:], -1.0, 1.0, ALU.mult, ALU.add)
                for n, r in enumerate(SPLIT):
                    pool.wait_ge(hi_ready, n + 1)
                    pool.tensor_tensor(w_lo[r][:], w_f[r][:], w_hi[r][:].bitcast(F32), ALU.subtract).then_inc(lo_ready, 1)

            @block.tensor
            def _(pe):
                pe.wait_ge(consts_loaded, 4 * 16)
                for c in range(F // P):
                    mm = pe.matmul(vfc[:, c, :], wfc_f[:, c * P:(c + 1) * P], afc_f[:], start=True, stop=True)
                mm.then_inc(vfc_done, 1)

            @block.vector
            def _(dve):
                dots = 0
                for r in range(ROUNDS):
                    if r == 2:
                        dve.wait_ge(vfc_done, 1)
                        dve.tensor_scalar(v_f[r][:, :, 0], vfc[:, :, 1], -1.0, None, ALU.mult).then_inc(dots_done, 1)
                        dve.tensor_scalar(v_f[r][:, :, 1], vfc[:, :, 0], -1.0, None, ALU.mult).then_inc(dots_done, 1)
                        dots += 2
                        continue
                    dve.wait_ge(w_loaded[r], 16)
                    dve.wait_ge(a_loaded[r], 16 if r < 2 else 2 * 16)
                    heads, width = (H, FH) if r == 3 else (1, F)
                    for c in range(v_f[r].shape[1]):
                        for k in range(NV[r]):
                            half_, head = k // heads, k % heads
                            if r == 1:
                                half_ = 1 - half_
                            a = a_b[r][:, half_ * heads * width + head * width:][:, 0:width]
                            if dots >= 2:
                                dve.wait_ge(dots_done, dots - 1)
                            dve.tensor_tensor_reduce(junk[:, dots % 2, 0:width], w_f[r][:, c, head * width:(head + 1) * width], a,
                                                     -1.0, 0.0, ALU.mult, ALU.add, v_f[r][:, c, k:k + 1]).then_inc(dots_done, 1)
                            dots += 1
                dve.wait_ge(dots_done, dots)
                for r in range(ROUNDS):
                    dve.wait_ge(v_hi_ready, r + 1)
                    dve.tensor_tensor(v_r[r][:, :, NV[r]:2 * NV[r]], v_f[r][:], v_r[r][:, :, 0:NV[r]].bitcast(F32), ALU.subtract)
                dve.wait_ge(consts_loaded, 4 * 16)
                dve.tensor_copy(sel_r[0:KSEL], sel_f[:])
                dve.memset(sel_r[KSEL:P].bitcast(F32), 0.0)
                dve.wait_ge(biases_loaded, 2 * 16)
                dve.tensor_scalar(bias4[:], bias4[:], -2.0, None, ALU.add)

        nc.clear_and_free_semaphores(setup_sems)
        nc.all_engine_barrier()


def gat_layers_kernel(nc, x, adj, w0, a0, w1, a1, wfc, afc, w3, as3, ad3, b3, w4, as4, ad4, b4,
                      ident, sel, out):
    B, N, F = x.shape
    H, FH = as3.shape
    HF = H * FH
    C = F // P
    C4 = HF // P
    assert N == P and F == 512 and HF == 2 * F and H == 4

    with ExitStack() as ctx:
        def sb(name, shape, dt=F32):
            return ctx.enter_context(nc.sbuf_tensor("sb_" + name, shape, dt))

        def bank(name):
            return ctx.enter_context(nc.psum_tensor("ps_" + name, [P, F], F32))

        def sem(name):
            return ctx.enter_context(nc.semaphore(name))

        eye, noteye = sb("eye", [P, P]), sb("noteye", [P, P])
        half = sb("half", [P, 1])
        eps = sb("eps", [P, 1])
        zero = sb("zero", [P, 1])
        sel_r = sb("sel_r", [P, 2 + 2 * H, P], F32R)
        W_SHAPE = [[P, C, F], [P, C, F], None, [P, C, HF], [P, C4, F]]
        w_hi = [sb(f"w{r}_hi", s, F32R) if s else None for r, s in enumerate(W_SHAPE)]
        w_lo = [sb(f"w{r}_lo", s, F32R) if s else None for r, s in enumerate(W_SHAPE)]
        NV = [2, 2, 2, 2 * H, 2]
        CH = [C, C, C, C, C4]
        v_f = [sb(f"v{r}_f", [P, CH[r], NV[r]]) for r in range(ROUNDS)]
        v_r = [sb(f"v{r}_r", [P, CH[r], 2 * NV[r]], F32R) for r in range(ROUNDS)]
        bias3 = sb("bias3", [P, HF])
        bias4 = sb("bias4", [P, F])

        prepare_weights(nc, (eye, noteye, half, eps, zero, sel_r, w_hi, w_lo, v_f, v_r, NV, bias3, bias4),
                        (w0, a0, w1, a1, wfc, afc, w3, as3, ad3, b3, w4, as4, ad4, b4, ident, sel))

        x_in = sb("x_in", [P, 2, F])
        x_mid = [sb(f"x_mid{r}", [P, 2, F]) for r in range(3)]
        x_out = sb("x_out", [P, 2, F])
        adj_i = sb("adj_i", [P, 2, P], I32)
        m_nat = sb("m_nat", [P, 2, P])
        m_le0 = sb("m_le0", [P, P])
        m_t = sb("m_t", [P, 2, P])
        m_self = sb("m_self", [P, 2, P])
        h4_hi = sb("h4_hi", [P, 2, C4 * P], F32R)
        h4_lo = sb("h4_lo", [P, 2, C4 * P], F32R)

        CHAIN = [0, 0, 1, 2, 3]

        def per_chain(name, shapes, dt=F32):
            return [sb(f"{name}_c{k}", s, dt) if s else None for k, s in enumerate(shapes)]

        HEADS = [1, 1, H, 1]
        st, mv, ve, nm, rstd = ([sb(f"{name}{r}", [P, n]) for r in range(4)] for name, n in (
            ("st", 6),
            ("mv", 2),
            ("ve", 1),
            ("nm", 1),
            ("rstd", 1)))
        xn = [sb(f"xn{r}", [P, F]) if r != 2 else None for r in range(4)]
        hT_hi = per_chain("hT_hi", [[P, F]] * 3, F32R)
        hT_lo = per_chain("hT_lo", [[P, F]] * 3, F32R)
        rows_r = per_chain("rows_r", [[P, P]] * 4, F32R)
        sc = per_chain("sc", [[P, n, P] for n in HEADS])
        mn = per_chain("mn", [[P, n] for n in HEADS])
        sm = per_chain("sm", [[P, n] for n in HEADS])
        rc = per_chain("rc", [[P, n] for n in HEADS])
        att_hi = per_chain("att_hi", [[P, 1, P], [P, 1, P], None, [P, 1, P]], F32R)
        att_lo = per_chain("att_lo", [[P, 1, P], [P, 1, P], None, [P, 1, P]], F32R)
        att3 = sb("att3", [P, H, P])
        tmp = per_chain("tmp", [[P, 1, F], [P, 1, F], [P, 2, F], None])
        VAL = [[P, F], [P, F], None, [P, F]]
        val_hi = per_chain("val_hi", VAL, F32R)
        val_lo = per_chain("val_lo", VAL, F32R)
        val3 = sb("val3", [P, HF])
        val0_f, h_nat = tmp[0][:, 0, :], tmp[1][:, 0, :]

        serial = [bank(f"serial{k}") for k in range(4)]
        mixed = [bank("mixed0"), serial[3], serial[1], None, bank("mixed4")]
        mixed3 = [bank("mixed3a"), bank("mixed3b")]

        def per_round(name, rounds=range(ROUNDS)):
            return [sem(f"{name}{r}") if r in rounds else None for r in range(ROUNDS)]

        LN = range(4)
        x_loaded = [sem("x_loaded0"), sem("x_loaded1")]
        adj_loaded = [sem("adj_loaded0"), sem("adj_loaded1")]
        out_stored = [sem("out_stored0"), sem("out_stored1")]
        masks_ready, m_le0_turned = sem("masks_ready"), sem("m_le0_turned")
        m_t_ready, m_self_ready = sem("m_t_ready"), sem("m_self_ready")
        stats_done = per_round("stats_done", LN)
        moments_ready = per_round("moments_ready", LN)
        vareps_ready = per_round("vareps_ready", LN)
        rstd_done = per_round("rstd_done", LN)
        rstd_ready = per_round("rstd_ready", LN)
        xn_ready = per_round("xn_ready", (0, 1, 3))
        h_nat_ready = sem("h_nat_ready")
        hT_turned = per_round("hT_turned", LN)
        hi_ready = per_round("hi_ready", LN)
        lo_ready = per_round("lo_ready", LN)
        rows_done = per_round("rows_done")
        rows_hi_ready = per_round("rows_hi_ready")
        rows_lo_ready = per_round("rows_lo_ready")
        z_done = per_round("z_done")
        z_copied = per_round("z_copied")
        leaky_done = per_round("leaky_done")
        max_done = per_round("max_done")
        exp_done = per_round("exp_done")
        recip_done = per_round("recip_done")
        norm_done = per_round("norm_done", range(1, 5))
        att_turned = per_round("att_turned", range(1, 5))
        att_ready = per_round("att_ready", (3,))
        att_hi_ready = per_round("att_hi_ready", (0, 1, 2, 4))
        att_lo_ready = per_round("att_lo_ready", (0, 1, 2, 4))
        prod_done = per_round("prod_done", (0, 1, 3, 4))
        prod3b_done = sem("prod3b_done")
        val_ready = per_round("val_ready", (4,))
        val_hi_ready = per_round("val_hi_ready", (0, 1, 2, 4))
        val_lo_ready = per_round("val_lo_ready", (0, 1, 2, 4))
        val3_ready = [sem("val3a_ready"), sem("val3b_ready")]
        mix_done = per_round("mix_done")
        neg_ready = per_round("neg_ready", range(3))
        elu_exp_ready = per_round("elu_exp_ready", (1, 2))
        resid_ready = per_round("resid_ready", range(3))
        x_ready = per_round("x_ready", (0, 1, 2, 4))
        mix3_done = [mix_done[3], sem("mix3b_done")]
        neg3_ready = [sem("neg3a_ready"), sem("neg3b_ready")]
        exp3_ready = [sem("exp3a_ready"), sem("exp3b_ready")]
        sum3_ready = [sem("sum3a_ready"), sem("sum3b_ready")]
        h4_hi_ready = [sem("h4_hi_a_ready"), sem("h4_hi_b_ready")]
        h4_lo_ready = [sem("h4_lo_a_ready"), sem("h4_lo_b_ready")]
        rows_cleared, wait_passed = sem("rows_cleared"), sem("wait_passed")

        block = ctx.enter_context(nc.Block())

        @block.sync
        def _(sp):
            def turn(g0, g1, g2, g3, g4, g5):
                if g0:
                    if g0.has_past(2):
                        sp.wait_ge(resid_ready[0], g0.count(back=2))
                    sp.dma_start(x_in[:, g0.slot, :], g0.row(x)).then_inc(x_loaded[g0.slot], 16)
                    if g0.has_past(2):
                        sp.wait_ge(masks_ready, g0.count(back=2))
                    sp.dma_start(adj_i[:, g0.slot, :], g0.row(adj)).then_inc(adj_loaded[g0.slot], 16)
                if g5:
                    sp.wait_ge(x_ready[4], g5.count())
                    sp.dma_start(g5.row(out), x_out[:, g5.slot, :]).then_inc(out_stored[g5.slot], 16)

            in_turns(sp, B, turn)
            for slot in range(2):
                sp.wait_ge(out_stored[slot], 16 * len(range(slot, B, 2)))

        @block.tensor
        def _(pe):
            def score_rows(r, hi, lo):
                for c in range(CH[r]):
                    for part in (hi, lo):
                        mm = pe.matmul(serial[CHAIN[r]][0:2 * NV[r], 0:P], v_r[r][:, c, :], part[:, c * P:(c + 1) * P],
                                       start=(c == 0 and part is hi), stop=(c == CH[r] - 1 and part is lo))
                return mm

            def product(r, hi, lo, c, q=0):
                a, b = hi[:, c * P:(c + 1) * P], lo[:, c * P:(c + 1) * P]
                wh, wl = w_hi[r][:, c, q * F:(q + 1) * F], w_lo[r][:, c, q * F:(q + 1) * F]
                dst = (mixed3[q] if r == 3 else mixed[r])[:]
                pe.matmul(dst, a, wh, start=(c == 0), stop=False)
                pe.matmul(dst, a, wl, start=False, stop=False)
                return pe.matmul(dst, b, wh, start=False, stop=(c == CH[r] - 1))

            def scores(k, heads, first):
                pe.matmul(serial[k][:, 0:heads * P], rows_r[k][:], sel_r[:, first + heads:first + 2 * heads, :],
                          start=True, stop=False)
                for h in range(heads):
                    mm = pe.matmul(serial[k][:, h * P:(h + 1) * P], sel_r[:, first + h, :], rows_r[k][:],
                                   start=False, stop=(h == heads - 1))
                return mm

            def mix(dst, k, h):
                pe.matmul(dst, att_hi[k][:, h, :], val_hi[k][:], start=True, stop=False)
                pe.matmul(dst, att_hi[k][:, h, :], val_lo[k][:], start=False, stop=False)
                return pe.matmul(dst, att_lo[k][:, h, :], val_hi[k][:], start=False, stop=True)

            def turn(g0, g1, g2, g3, g4, g5):
                if g2:
                    pe.wait_ge(m_t_ready, g2.count())
                    for c in range(C):
                        mm = pe.transpose(serial[0][:, c * P:(c + 1) * P], xn[0][:, c * P:(c + 1) * P], eye[:])
                    mm.then_inc(hT_turned[0], 1)
                if g3:
                    pe.wait_ge(att_lo_ready[1], g3.count())
                    pe.wait_ge(val_lo_ready[1], g3.count())
                    mix(mixed[1][:], 0, 0).then_inc(mix_done[1], 1)
                if g5:
                    pe.wait_ge(val3_ready[1], g5.count())
                    for f in range(C, 2 * C):
                        mm = pe.matmul(mixed3[1][:, f % C * P:(f % C + 1) * P], val3[:, f * P:(f + 1) * P],
                                       att3[:, f * P // FH, :], start=True, stop=True)
                    mm.then_inc(mix3_done[1], 1)
                if g4:
                    pe.wait_ge(xn_ready[3], g4.count())
                    for c in range(C):
                        mm = pe.transpose(serial[2][:, c * P:(c + 1) * P], xn[3][:, c * P:(c + 1) * P], eye[:])
                    mm.then_inc(hT_turned[3], 1)
                if g2:
                    pe.wait_ge(lo_ready[0], g2.count())
                    score_rows(0, hT_hi[0], hT_lo[0]).then_inc(rows_done[0], 1)
                if g2:
                    for c in range(0, 3):
                        mm = product(0, hT_hi[0], hT_lo[0], c)
                if g2:
                    pe.wait_ge(rows_lo_ready[0], g2.count())
                    scores(0, 1, 0).then_inc(z_done[0], 1)
                if g2:
                    product(0, hT_hi[0], hT_lo[0], 3).then_inc(prod_done[0], 1)
                if g4:
                    pe.wait_ge(lo_ready[3], g4.count())
                    score_rows(3, hT_hi[2], hT_lo[2]).then_inc(rows_done[3], 1)
                if g4:
                    for c in range(0, 4):
                        mm = product(3, hT_hi[2], hT_lo[2], c, q=0)
                    mm.then_inc(prod_done[3], 1)
                if g4:
                    pe.wait_ge(rows_lo_ready[3], g4.count())
                    scores(2, H, 2).then_inc(z_done[3], 1)
                if g3:
                    pe.wait_ge(h_nat_ready, g3.count())
                    for c in range(C):
                        mm = pe.transpose(serial[1][:, c * P:(c + 1) * P], h_nat[:, c * P:(c + 1) * P], eye[:])
                    mm.then_inc(hT_turned[2], 1)
                if g2:
                    pe.wait_ge(att_lo_ready[0], g2.count())
                    pe.wait_ge(val_lo_ready[0], g2.count())
                    mix(mixed[0][:], 0, 0).then_inc(mix_done[0], 1)
                if g5:
                    pe.wait_ge(h4_lo_ready[1], g5.count())
                    score_rows(4, h4_hi[:, g5.slot], h4_lo[:, g5.slot]).then_inc(rows_done[4], 1)
                if g5:
                    product(4, h4_hi[:, g5.slot], h4_lo[:, g5.slot], 0)
                if g3:
                    pe.wait_ge(lo_ready[2], g3.count())
                    score_rows(2, hT_hi[1], hT_lo[1]).then_inc(rows_done[2], 1)
                if g5:
                    for c in range(1, 3):
                        mm = product(4, h4_hi[:, g5.slot], h4_lo[:, g5.slot], c)
                if g3:
                    pe.wait_ge(rows_lo_ready[2], g3.count())
                    scores(1, 1, 0).then_inc(z_done[2], 1)
                if g5:
                    pe.wait_ge(rows_lo_ready[4], g5.count())
                    scores(3, 1, 0).then_inc(z_done[4], 1)
                if g5:
                    for c in range(3, 8):
                        mm = product(4, h4_hi[:, g5.slot], h4_lo[:, g5.slot], c)
                    mm.then_inc(prod_done[4], 1)
                if g3:
                    pe.wait_ge(norm_done[2], g3.count())
                    pe.transpose(serial[1][:, 0:P], sc[1][:, 0, :], eye[:]).then_inc(att_turned[2], 1)
                if g2:
                    pe.wait_ge(xn_ready[1], g2.count())
                    for c in range(C):
                        mm = pe.transpose(serial[0][:, c * P:(c + 1) * P], xn[1][:, c * P:(c + 1) * P], eye[:])
                    mm.then_inc(hT_turned[1], 1)
                if g4:
                    pe.wait_ge(norm_done[3], g4.count())
                    for h in range(H):
                        mm = pe.transpose(serial[2][:, h * P:(h + 1) * P], sc[2][:, h, :], eye[:])
                    mm.then_inc(att_turned[3], 1)
                if g5:
                    pe.wait_ge(norm_done[4], g5.count())
                    pe.transpose(serial[3][:, 0:P], sc[3][:, 0, :], eye[:]).then_inc(att_turned[4], 1)
                if g4:
                    product(3, hT_hi[2], hT_lo[2], 0, q=1)
                if g3:
                    pe.wait_ge(att_lo_ready[2], g3.count())
                    pe.wait_ge(val_lo_ready[2], g3.count())
                    mix(mixed[2][:], 1, 0).then_inc(mix_done[2], 1)
                if g2:
                    pe.wait_ge(lo_ready[1], g2.count())
                    score_rows(1, hT_hi[0], hT_lo[0]).then_inc(rows_done[1], 1)
                if g2:
                    if g2.has_past(3):
                        pe.wait_ge(att_lo_ready[4], g2.count(back=3))
                    for c in range(0, 2):
                        mm = product(1, hT_hi[0], hT_lo[0], c)
                if g2:
                    pe.wait_ge(rows_lo_ready[1], g2.count())
                    scores(0, 1, 0).then_inc(z_done[1], 1)
                if g5:
                    pe.wait_ge(att_lo_ready[4], g5.count())
                    pe.wait_ge(val_lo_ready[4], g5.count())
                    mix(mixed[4][:], 3, 0).then_inc(mix_done[4], 1)
                if g2:
                    for c in range(2, 4):
                        mm = product(1, hT_hi[0], hT_lo[0], c)
                    mm.then_inc(prod_done[1], 1)
                if g4:
                    pe.wait_ge(att_ready[3], g4.count())
                    pe.wait_ge(val3_ready[0], g4.count())
                    for f in range(C):
                        mm = pe.matmul(mixed3[0][:, f % C * P:(f % C + 1) * P], val3[:, f * P:(f + 1) * P],
                                       att3[:, f * P // FH, :], start=True, stop=True)
                    mm.then_inc(mix3_done[0], 1)
                if g2:
                    pe.wait_ge(norm_done[1], g2.count())
                    pe.transpose(serial[0][:, 0:P], sc[0][:, 0, :], eye[:]).then_inc(att_turned[1], 1)
                if g4:
                    for c in range(1, 3):
                        mm = product(3, hT_hi[2], hT_lo[2], c, q=1)
                if g1:
                    pe.wait_ge(masks_ready, g1.count())
                    if g1.has_past(1):
                        pe.wait_ge(att_lo_ready[1], g1.count(back=1))
                    pe.transpose(serial[0][:, 0:P], m_le0[:], eye[:]).then_inc(m_le0_turned, 1)
                if g4:
                    product(3, hT_hi[2], hT_lo[2], 3, q=1).then_inc(prod3b_done, 1)

            pe.wait_ge(rows_cleared, 4)
            in_turns(pe, B, turn)

        @block.scalar
        def _(act):
            def exp_rows(k, h):
                return act.activation(sc[k][:, h, :], sc[k][:, h, :], ACT.Exp, scale=-1.0,
                                      bias=mn[k][:, h:h + 1], accum_out=sm[k][:, h:h + 1])

            def turn(g0, g1, g2, g3, g4, g5):
                if g5:
                    act.wait_ge(neg3_ready[0], g5.count())
                    act.activation(tmp[2][:, 0, :], tmp[2][:, 0, :], ACT.Exp, scale=-1.0).then_inc(exp3_ready[0], 1)
                if g2:
                    act.wait_ge(hT_turned[0], g2.count())
                    act.activation(hT_hi[0][:], serial[0][:], ACT.Copy).then_inc(hi_ready[0], 1)
                if g4:
                    act.wait_ge(rstd_ready[3], g4.count())
                    act.activation(xn[3][:], x_mid[2][:, g4.slot, :], ACT.Relu, scale=rstd[3][:], bias=nm[3][:]).then_inc(xn_ready[3], 1)
                if g3:
                    act.wait_ge(mix_done[1], g3.count())
                    act.activation(tmp[0][:, 0, :], mixed[1][:], ACT.Relu, scale=-1.0).then_inc(neg_ready[1], 1)
                if g3:
                    act.wait_ge(neg_ready[1], g3.count())
                    act.activation(tmp[0][:, 0, :], tmp[0][:, 0, :], ACT.Exp, scale=-1.0).then_inc(elu_exp_ready[1], 1)
                if g4:
                    act.wait_ge(hT_turned[3], g4.count())
                    act.activation(hT_hi[2][:], serial[2][:], ACT.Copy).then_inc(hi_ready[3], 1)
                if g5:
                    act.wait_ge(mix3_done[1], g5.count())
                    act.activation(tmp[2][:, 1, :], mixed3[1][:], ACT.Relu, scale=-1.0).then_inc(neg3_ready[1], 1)
                if g2:
                    act.wait_ge(rows_done[0], g2.count())
                    act.activation(rows_r[0][0:2 * NV[0], :], serial[0][0:2 * NV[0], 0:P], ACT.Copy).then_inc(rows_hi_ready[0], 1)
                if g5:
                    act.wait_ge(neg3_ready[1], g5.count())
                    act.activation(tmp[2][:, 1, :], tmp[2][:, 1, :], ACT.Exp, scale=-1.0).then_inc(exp3_ready[1], 1)
                if g5:
                    act.wait_ge(sum3_ready[0], g5.count())
                    act.activation(h4_hi[:, g5.slot, 0:F], tmp[2][:, 0, :], ACT.Copy, bias=-1.0).then_inc(h4_hi_ready[0], 1)
                if g2:
                    act.wait_ge(z_done[0], g2.count())
                    act.activation(sc[0][:].rearrange("p h n -> p (h n)"), serial[0][:, 0:P], ACT.Copy).then_inc(z_copied[0], 1)
                if g2:
                    act.wait_ge(prod_done[0], g2.count())
                    if g2.has_past(1):
                        act.wait_ge(x_ready[1], g2.count(back=1))
                    act.activation(val0_f[:], mixed[0][:], ACT.Copy)
                    act.activation(val_hi[0][:], mixed[0][:], ACT.Copy).then_inc(val_hi_ready[0], 1)
                if g4:
                    act.wait_ge(rows_done[3], g4.count())
                    act.activation(rows_r[2][0:2 * NV[3], :], serial[2][0:2 * NV[3], 0:P], ACT.Copy).then_inc(rows_hi_ready[3], 1)
                if g5:
                    act.wait_ge(sum3_ready[1], g5.count())
                    act.activation(h4_hi[:, g5.slot, F:2 * F], tmp[2][:, 1, :], ACT.Copy, bias=-1.0).then_inc(h4_hi_ready[1], 1)
                if g2:
                    act.wait_ge(max_done[0], g2.count())
                    exp_rows(0, 0).then_inc(exp_done[0], 1)
                if g3:
                    act.wait_ge(rstd_ready[2], g3.count())
                    act.activation(h_nat[:], x_mid[1][:, g3.slot, :], ACT.Relu, scale=rstd[2][:], bias=nm[2][:]).then_inc(h_nat_ready, 1)
                if g4:
                    act.wait_ge(z_done[3], g4.count())
                    act.activation(sc[2][:].rearrange("p h n -> p (h n)"), serial[2][:, 0:H * P], ACT.Copy).then_inc(z_copied[3], 1)
                if g3:
                    act.wait_ge(hT_turned[2], g3.count())
                    act.activation(hT_hi[1][:], serial[1][:], ACT.Copy).then_inc(hi_ready[2], 1)
                if g2:
                    act.wait_ge(mix_done[0], g2.count())
                    act.activation(tmp[0][:, 0, :], mixed[0][:], ACT.Relu, scale=-SLOPE).then_inc(neg_ready[0], 1)
                if g5:
                    act.wait_ge(rows_done[4], g5.count())
                    act.activation(rows_r[3][0:2 * NV[4], :], serial[3][0:2 * NV[4], 0:P], ACT.Copy).then_inc(rows_hi_ready[4], 1)
                if g3:
                    act.wait_ge(rows_done[2], g3.count())
                    act.activation(rows_r[1][0:2 * NV[2], :], serial[1][0:2 * NV[2], 0:P], ACT.Copy).then_inc(rows_hi_ready[2], 1)
                if g4:
                    act.wait_ge(max_done[3], g4.count())
                    for h in range(H):
                        ins = exp_rows(2, h)
                    ins.then_inc(exp_done[3], 1)
                if g3:
                    act.wait_ge(z_done[2], g3.count())
                    act.activation(sc[1][:].rearrange("p h n -> p (h n)"), serial[1][:, 0:P], ACT.Copy).then_inc(z_copied[2], 1)
                if g5:
                    act.wait_ge(z_done[4], g5.count())
                    act.activation(sc[3][:].rearrange("p h n -> p (h n)"), serial[3][:, 0:P], ACT.Copy).then_inc(z_copied[4], 1)
                if g3:
                    act.activation(val_hi[1][:], h_nat[:], ACT.Copy).then_inc(val_hi_ready[2], 1)
                if g3:
                    act.wait_ge(max_done[2], g3.count())
                    exp_rows(1, 0).then_inc(exp_done[2], 1)
                if g2:
                    act.wait_ge(rstd_ready[1], g2.count())
                    act.activation(xn[1][:], x_mid[0][:, g2.slot, :], ACT.Relu, scale=rstd[1][:], bias=nm[1][:]).then_inc(xn_ready[1], 1)
                if g5:
                    act.wait_ge(max_done[4], g5.count())
                    exp_rows(3, 0).then_inc(exp_done[4], 1)
                if g3:
                    act.wait_ge(att_turned[2], g3.count())
                    act.activation(att_hi[1][:].rearrange("p h n -> p (h n)"), serial[1][:, 0:P], ACT.Copy).then_inc(att_hi_ready[2], 1)
                if g2:
                    act.wait_ge(hT_turned[1], g2.count())
                    act.activation(hT_hi[0][:], serial[0][:], ACT.Copy).then_inc(hi_ready[1], 1)
                if g5:
                    act.wait_ge(att_turned[4], g5.count())
                    act.activation(att_hi[3][:].rearrange("p h n -> p (h n)"), serial[3][:, 0:P], ACT.Copy).then_inc(att_hi_ready[4], 1)
                if g5:
                    act.wait_ge(val_ready[4], g5.count())
                    act.activation(val_hi[3][:], x_out[:, g5.slot, :], ACT.Copy).then_inc(val_hi_ready[4], 1)
                if g4:
                    act.wait_ge(att_turned[3], g4.count())
                    act.activation(att3[:].rearrange("p h n -> p (h n)"), serial[2][:, 0:H * P], ACT.Copy).then_inc(att_ready[3], 1)
                if g3:
                    act.wait_ge(mix_done[2], g3.count())
                    act.activation(tmp[1][:, 0, :], mixed[2][:], ACT.Relu, scale=-1.0).then_inc(neg_ready[2], 1)
                if g2:
                    act.wait_ge(rows_done[1], g2.count())
                    act.activation(rows_r[0][0:2 * NV[1], :], serial[0][0:2 * NV[1], 0:P], ACT.Copy).then_inc(rows_hi_ready[1], 1)
                if g2:
                    act.wait_ge(z_done[1], g2.count())
                    act.activation(sc[0][:].rearrange("p h n -> p (h n)"), serial[0][:, 0:P], ACT.Copy).then_inc(z_copied[1], 1)
                if g3:
                    act.wait_ge(neg_ready[2], g3.count())
                    act.activation(tmp[1][:, 0, :], tmp[1][:, 0, :], ACT.Exp, scale=-1.0).then_inc(elu_exp_ready[2], 1)
                if g2:
                    act.wait_ge(max_done[1], g2.count())
                    exp_rows(0, 0).then_inc(exp_done[1], 1)
                if g2:
                    act.wait_ge(prod_done[1], g2.count())
                    act.activation(val0_f[:], mixed[1][:], ACT.Copy)
                    act.activation(val_hi[0][:], mixed[1][:], ACT.Copy).then_inc(val_hi_ready[1], 1)
                if g2:
                    act.wait_ge(att_turned[1], g2.count())
                    act.activation(att_hi[0][:].rearrange("p h n -> p (h n)"), serial[0][:, 0:P], ACT.Copy).then_inc(att_hi_ready[1], 1)
                if g4:
                    act.wait_ge(mix3_done[0], g4.count())
                    act.activation(tmp[2][:, 0, :], mixed3[0][:], ACT.Relu, scale=-1.0).then_inc(neg3_ready[0], 1)
                if g1:
                    act.wait_ge(rstd_ready[0], g1.count())
                    act.activation(xn[0][:], x_in[:, g1.slot, :], ACT.Relu, scale=rstd[0][:], bias=nm[0][:]).then_inc(xn_ready[0], 1)
                if g1:
                    act.wait_ge(m_le0_turned, g1.count())
                    act.activation(m_t[:, g1.slot, :], serial[0][:, 0:P], ACT.Copy).then_inc(m_t_ready, 1)

            in_turns(act, B, turn)

        @block.gpsimd
        def _(pool):
            def turn(g0, g1, g2, g3, g4, g5):
                if g3:
                    pool.wait_ge(elu_exp_ready[1], g3.count())
                    pool.tensor_tensor(tmp[0][:, 0, :], x_mid[0][:, g3.slot, :], tmp[0][:, 0, :], ALU.add).then_inc(resid_ready[1], 1)
                if g3:
                    pool.wait_ge(moments_ready[2], g3.count())
                    pool.tensor_tensor(ve[2][:], mv[2][:, 1:2], eps[:], ALU.add)
                    pool.tensor_tensor(nm[2][:], zero[:], mv[2][:, 0:1], ALU.subtract).then_inc(vareps_ready[2], 1)
                    pool.wait_ge(vareps_ready[2], g3.count())
                    pool.tensor_tensor(rstd[2][:], ve[2][:], half[:], ALU.pow).then_inc(rstd_done[2], 1)
                    pool.wait_ge(rstd_done[2], g3.count())
                    pool.tensor_tensor(nm[2][:], nm[2][:], rstd[2][:], ALU.mult).then_inc(rstd_ready[2], 1)
                if g2:
                    pool.wait_ge(val_hi_ready[0], g2.count())
                    pool.tensor_tensor(val_lo[0][:], val0_f[:], val_hi[0][:].bitcast(F32), ALU.subtract).then_inc(val_lo_ready[0], 1)
                if g2:
                    pool.wait_ge(neg_ready[0], g2.count())
                    pool.tensor_tensor(tmp[0][:, 0, :], x_in[:, g2.slot, :], tmp[0][:, 0, :], ALU.subtract).then_inc(resid_ready[0], 1)
                if g2:
                    pool.wait_ge(moments_ready[1], g2.count())
                    pool.tensor_tensor(ve[1][:], mv[1][:, 1:2], eps[:], ALU.add)
                    pool.tensor_tensor(nm[1][:], zero[:], mv[1][:, 0:1], ALU.subtract).then_inc(vareps_ready[1], 1)
                    pool.wait_ge(vareps_ready[1], g2.count())
                    pool.tensor_tensor(rstd[1][:], ve[1][:], half[:], ALU.pow).then_inc(rstd_done[1], 1)
                    pool.wait_ge(rstd_done[1], g2.count())
                    pool.tensor_tensor(nm[1][:], nm[1][:], rstd[1][:], ALU.mult).then_inc(rstd_ready[1], 1)
                if g4:
                    pool.wait_ge(recip_done[3], g4.count())
                    pool.tensor_tensor(sc[2][:], sc[2][:], rc[2][:].rearrange("p (h o) -> p h o", o=1).broadcast_to([P, H, P]),
                                       ALU.mult).then_inc(norm_done[3], 1)
                if g3:
                    pool.wait_ge(val_hi_ready[2], g3.count())
                    pool.tensor_tensor(val_lo[1][:], h_nat[:], val_hi[1][:].bitcast(F32), ALU.subtract).then_inc(val_lo_ready[2], 1)
                if g3:
                    if g3.has_past(2):
                        pool.wait_ge(max_done[4], g3.count(back=2))
                    pool.tensor_tensor(m_self[:, g3.slot, :], m_t[:, g3.slot, :], noteye[:], ALU.mult).then_inc(m_self_ready, 1)
                if g5:
                    pool.wait_ge(val_hi_ready[4], g5.count())
                    pool.tensor_tensor(val_lo[3][:], x_out[:, g5.slot, :], val_hi[3][:].bitcast(F32), ALU.subtract).then_inc(val_lo_ready[4], 1)
                if g1:
                    pool.wait_ge(moments_ready[0], g1.count())
                    pool.tensor_tensor(ve[0][:], mv[0][:, 1:2], eps[:], ALU.add)
                    pool.tensor_tensor(nm[0][:], zero[:], mv[0][:, 0:1], ALU.subtract).then_inc(vareps_ready[0], 1)
                    pool.wait_ge(vareps_ready[0], g1.count())
                    pool.tensor_tensor(rstd[0][:], ve[0][:], half[:], ALU.pow).then_inc(rstd_done[0], 1)
                    pool.wait_ge(rstd_done[0], g1.count())
                    pool.tensor_tensor(nm[0][:], nm[0][:], rstd[0][:], ALU.mult).then_inc(rstd_ready[0], 1)
                if g3:
                    pool.wait_ge(elu_exp_ready[2], g3.count())
                    pool.tensor_tensor(tmp[1][:, 0, :], x_mid[1][:, g3.slot, :], tmp[1][:, 0, :], ALU.add).then_inc(resid_ready[2], 1)
                if g2:
                    pool.wait_ge(val_hi_ready[1], g2.count())
                    pool.tensor_tensor(val_lo[0][:], val0_f[:], val_hi[0][:].bitcast(F32), ALU.subtract).then_inc(val_lo_ready[1], 1)
                if g3:
                    pool.wait_ge(moments_ready[3], g3.count())
                    pool.tensor_tensor(ve[3][:], mv[3][:, 1:2], eps[:], ALU.add)
                    pool.tensor_tensor(nm[3][:], zero[:], mv[3][:, 0:1], ALU.subtract).then_inc(vareps_ready[3], 1)
                    pool.wait_ge(vareps_ready[3], g3.count())
                    pool.tensor_tensor(rstd[3][:], ve[3][:], half[:], ALU.pow).then_inc(rstd_done[3], 1)
                    pool.wait_ge(rstd_done[3], g3.count())
                    pool.tensor_tensor(nm[3][:], nm[3][:], rstd[3][:], ALU.mult).then_inc(rstd_ready[3], 1)

            in_turns(pool, B, turn)

        @block.vector
        def _(dve):
            def masked_min(k, h, mask):
                return dve.tensor_tensor_reduce(sc[k][:, h, :], sc[k][:, h, :], mask, 1.0, 3.0e38,
                                                ALU.add, ALU.min, mn[k][:, h:h + 1])

            def turn(g0, g1, g2, g3, g4, g5):
                if g5:
                    dve.wait_ge(prod3b_done, g5.count())
                    dve.tensor_tensor(val3[:, F:2 * F], mixed3[1][:], bias3[:, F:2 * F], ALU.add).then_inc(val3_ready[1], 1)
                if g2:
                    dve.wait_ge(hi_ready[0], g2.count())
                    dve.tensor_tensor(hT_lo[0][:], serial[0][:], hT_hi[0][:].bitcast(F32), ALU.subtract).then_inc(lo_ready[0], 1)
                if g1:
                    dve.wait_ge(x_loaded[g1.slot], g1.dma_count())
                    dve.bn_stats(st[0][:], x_in[:, g1.slot, :]).then_inc(stats_done[0], 1)
                if g5:
                    dve.wait_ge(exp3_ready[0], g5.count())
                    dve.scalar_tensor_tensor(out=tmp[2][:, 0, :], in0=mixed3[0][:], scalar=0.0, in1=tmp[2][:, 0, :],
                                             op0=ALU.max, op1=ALU.add).then_inc(sum3_ready[0], 1)
                if g4:
                    dve.wait_ge(hi_ready[3], g4.count())
                    dve.tensor_tensor(hT_lo[2][:], serial[2][:], hT_hi[2][:].bitcast(F32), ALU.subtract).then_inc(lo_ready[3], 1)
                if g2:
                    dve.wait_ge(rows_hi_ready[0], g2.count())
                    dve.tensor_tensor(rows_r[0][LOROW:LOROW + 2 * NV[0], :], serial[0][0:2 * NV[0], 0:P], rows_r[0][0:2 * NV[0], :].bitcast(F32),
                                      ALU.subtract).then_inc(rows_lo_ready[0], 1)
                if g3:
                    dve.wait_ge(resid_ready[1], g3.count())
                    dve.scalar_tensor_tensor(out=x_mid[1][:, g3.slot, :], in0=mixed[1][:], scalar=0.0, in1=tmp[0][:, 0, :],
                                             op0=ALU.max, op1=ALU.add).then_inc(x_ready[1], 1)
                if g3:
                    dve.wait_ge(x_ready[1], g3.count())
                    dve.bn_stats(st[2][:], x_mid[1][:, g3.slot, :]).then_inc(stats_done[2], 1)
                if g3:
                    dve.wait_ge(stats_done[2], g3.count())
                    dve.sem_inc(wait_passed, 1)
                    dve.bn_aggr(mv[2][:], st[2][:]).then_inc(moments_ready[2], 1)
                if g2:
                    dve.wait_ge(z_copied[0], g2.count())
                    dve.scalar_tensor_tensor(out=sc[0][:], in0=sc[0][:], scalar=SLOPE, in1=sc[0][:],
                                             op0=ALU.mult, op1=ALU.min).then_inc(leaky_done[0], 1)
                if g5:
                    dve.wait_ge(exp3_ready[1], g5.count())
                    dve.scalar_tensor_tensor(out=tmp[2][:, 1, :], in0=mixed3[1][:], scalar=0.0, in1=tmp[2][:, 1, :],
                                             op0=ALU.max, op1=ALU.add).then_inc(sum3_ready[1], 1)
                if g2:
                    dve.wait_ge(leaky_done[0], g2.count())
                    dve.sem_inc(wait_passed, 1)
                    masked_min(0, 0, m_t[:, g2.slot, :]).then_inc(max_done[0], 1)
                if g5:
                    dve.wait_ge(h4_hi_ready[0], g5.count())
                    dve.scalar_tensor_tensor(out=h4_lo[:, g5.slot, 0:F], in0=tmp[2][:, 0, :], scalar=-1.0,
                                             in1=h4_hi[:, g5.slot, 0:F].bitcast(F32),
                                             op0=ALU.add, op1=ALU.subtract).then_inc(h4_lo_ready[0], 1)
                if g4:
                    dve.wait_ge(rows_hi_ready[3], g4.count())
                    dve.tensor_tensor(rows_r[2][LOROW:LOROW + 2 * NV[3], :], serial[2][0:2 * NV[3], 0:P], rows_r[2][0:2 * NV[3], :].bitcast(F32),
                                      ALU.subtract).then_inc(rows_lo_ready[3], 1)
                if g2:
                    dve.wait_ge(exp_done[0], g2.count())
                    dve.reciprocal(rc[0][:], sm[0][:]).then_inc(recip_done[0], 1)
                if g2:
                    dve.wait_ge(recip_done[0], g2.count())
                    dve.tensor_scalar(att_hi[0][:, 0, :], sc[0][:, 0, :], rc[0][:], None, ALU.mult).then_inc(att_hi_ready[0], 1)
                if g2:
                    dve.wait_ge(att_hi_ready[0], g2.count())
                    dve.scalar_tensor_tensor(out=att_lo[0][:, 0, :], in0=sc[0][:, 0, :], scalar=rc[0][:], in1=att_hi[0][:, 0, :].bitcast(F32),
                                             op0=ALU.mult, op1=ALU.subtract).then_inc(att_lo_ready[0], 1)
                if g5:
                    dve.wait_ge(h4_hi_ready[1], g5.count())
                    dve.scalar_tensor_tensor(out=h4_lo[:, g5.slot, F:2 * F], in0=tmp[2][:, 1, :], scalar=-1.0,
                                             in1=h4_hi[:, g5.slot, F:2 * F].bitcast(F32),
                                             op0=ALU.add, op1=ALU.subtract).then_inc(h4_lo_ready[1], 1)
                if g4:
                    dve.wait_ge(z_copied[3], g4.count())
                    dve.scalar_tensor_tensor(out=sc[2][:], in0=sc[2][:], scalar=SLOPE, in1=sc[2][:],
                                             op0=ALU.mult, op1=ALU.min).then_inc(leaky_done[3], 1)
                if g3:
                    dve.wait_ge(hi_ready[2], g3.count())
                    dve.tensor_tensor(hT_lo[1][:], serial[1][:], hT_hi[1][:].bitcast(F32), ALU.subtract).then_inc(lo_ready[2], 1)
                if g1:
                    dve.wait_ge(stats_done[0], g1.count())
                    dve.sem_inc(wait_passed, 1)
                    dve.bn_aggr(mv[0][:], st[0][:]).then_inc(moments_ready[0], 1)
                if g4:
                    dve.wait_ge(leaky_done[3], g4.count())
                    dve.sem_inc(wait_passed, 1)
                    for h in range(H):
                        ins = masked_min(2, h, m_self[:, g4.slot, :])
                    ins.then_inc(max_done[3], 1)
                if g5:
                    dve.wait_ge(rows_hi_ready[4], g5.count())
                    dve.tensor_tensor(rows_r[3][LOROW:LOROW + 2 * NV[4], :], serial[3][0:2 * NV[4], 0:P], rows_r[3][0:2 * NV[4], :].bitcast(F32),
                                      ALU.subtract).then_inc(rows_lo_ready[4], 1)
                if g2:
                    dve.wait_ge(resid_ready[0], g2.count())
                    dve.scalar_tensor_tensor(out=x_mid[0][:, g2.slot, :], in0=mixed[0][:], scalar=0.0, in1=tmp[0][:, 0, :],
                                             op0=ALU.max, op1=ALU.add).then_inc(x_ready[0], 1)
                if g3:
                    dve.wait_ge(rows_hi_ready[2], g3.count())
                    dve.tensor_tensor(rows_r[1][LOROW:LOROW + 2 * NV[2], :], serial[1][0:2 * NV[2], 0:P], rows_r[1][0:2 * NV[2], :].bitcast(F32),
                                      ALU.subtract).then_inc(rows_lo_ready[2], 1)
                if g2:
                    dve.wait_ge(x_ready[0], g2.count())
                    dve.bn_stats(st[1][:], x_mid[0][:, g2.slot, :]).then_inc(stats_done[1], 1)
                if g2:
                    dve.wait_ge(stats_done[1], g2.count())
                    dve.sem_inc(wait_passed, 1)
                    dve.bn_aggr(mv[1][:], st[1][:]).then_inc(moments_ready[1], 1)
                if g4:
                    dve.wait_ge(exp_done[3], g4.count())
                    dve.reciprocal(rc[2][:], sm[2][:]).then_inc(recip_done[3], 1)
                if g3:
                    dve.wait_ge(z_copied[2], g3.count())
                    dve.scalar_tensor_tensor(out=sc[1][:], in0=sc[1][:], scalar=SLOPE, in1=sc[1][:],
                                             op0=ALU.mult, op1=ALU.min).then_inc(leaky_done[2], 1)
                if g3:
                    dve.wait_ge(leaky_done[2], g3.count())
                    dve.sem_inc(wait_passed, 1)
                    masked_min(1, 0, m_nat[:, g3.slot, :]).then_inc(max_done[2], 1)
                if g1:
                    dve.wait_ge(adj_loaded[g1.slot], g1.dma_count())
                    if g1.has_past(2):
                        dve.wait_ge(max_done[2], g1.count(back=2))
                    dve.tensor_scalar(m_nat[:, g1.slot, :], adj_i[:, g1.slot, :], 0, BIG, ALU.is_equal, ALU.mult)
                    dve.tensor_scalar(m_le0[:], adj_i[:, g1.slot, :], 0, BIG, ALU.is_le, ALU.mult).then_inc(masks_ready, 1)
                if g5:
                    dve.wait_ge(z_copied[4], g5.count())
                    dve.scalar_tensor_tensor(out=sc[3][:], in0=sc[3][:], scalar=SLOPE, in1=sc[3][:],
                                             op0=ALU.mult, op1=ALU.min).then_inc(leaky_done[4], 1)
                if g5:
                    dve.wait_ge(leaky_done[4], g5.count())
                    dve.sem_inc(wait_passed, 1)
                    masked_min(3, 0, m_self[:, g5.slot, :]).then_inc(max_done[4], 1)
                if g3:
                    dve.wait_ge(exp_done[2], g3.count())
                    dve.reciprocal(rc[1][:], sm[1][:]).then_inc(recip_done[2], 1)
                if g3:
                    dve.wait_ge(recip_done[2], g3.count())
                    dve.tensor_scalar(sc[1][:, 0, :], sc[1][:, 0, :], rc[1][:], None, ALU.mult).then_inc(norm_done[2], 1)
                if g5:
                    dve.wait_ge(exp_done[4], g5.count())
                    dve.reciprocal(rc[3][:], sm[3][:]).then_inc(recip_done[4], 1)
                if g5:
                    dve.wait_ge(recip_done[4], g5.count())
                    dve.tensor_scalar(sc[3][:, 0, :], sc[3][:, 0, :], rc[3][:], None, ALU.mult).then_inc(norm_done[4], 1)
                if g5:
                    dve.wait_ge(prod_done[4], g5.count())
                    if g5.has_past(2):
                        dve.wait_ge(out_stored[g5.slot], g5.dma_count(back=2))
                    dve.tensor_tensor(x_out[:, g5.slot, :], mixed[4][:], bias4[:], ALU.add).then_inc(val_ready[4], 1)
                if g3:
                    dve.wait_ge(att_hi_ready[2], g3.count())
                    dve.tensor_tensor(att_lo[1][:].rearrange("p h n -> p (h n)"), serial[1][:, 0:P], att_hi[1][:].rearrange("p h n -> p (h n)").bitcast(F32),
                                      ALU.subtract).then_inc(att_lo_ready[2], 1)
                if g2:
                    dve.wait_ge(hi_ready[1], g2.count())
                    dve.tensor_tensor(hT_lo[0][:], serial[0][:], hT_hi[0][:].bitcast(F32), ALU.subtract).then_inc(lo_ready[1], 1)
                if g5:
                    dve.wait_ge(att_hi_ready[4], g5.count())
                    dve.tensor_tensor(att_lo[3][:].rearrange("p h n -> p (h n)"), serial[3][:, 0:P], att_hi[3][:].rearrange("p h n -> p (h n)").bitcast(F32),
                                      ALU.subtract).then_inc(att_lo_ready[4], 1)
                if g4:
                    dve.tensor_tensor(val3[:, 0:F], mixed3[0][:], bias3[:, 0:F], ALU.add).then_inc(val3_ready[0], 1)
                if g2:
                    dve.wait_ge(rows_hi_ready[1], g2.count())
                    dve.tensor_tensor(rows_r[0][LOROW:LOROW + 2 * NV[1], :], serial[0][0:2 * NV[1], 0:P], rows_r[0][0:2 * NV[1], :].bitcast(F32),
                                      ALU.subtract).then_inc(rows_lo_ready[1], 1)
                if g2:
                    dve.wait_ge(z_copied[1], g2.count())
                    dve.scalar_tensor_tensor(out=sc[0][:], in0=sc[0][:], scalar=SLOPE, in1=sc[0][:],
                                             op0=ALU.mult, op1=ALU.min).then_inc(leaky_done[1], 1)
                if g2:
                    dve.wait_ge(leaky_done[1], g2.count())
                    dve.sem_inc(wait_passed, 1)
                    masked_min(0, 0, m_nat[:, g2.slot, :]).then_inc(max_done[1], 1)
                if g5:
                    dve.wait_ge(mix_done[4], g5.count())
                    dve.tensor_tensor(x_out[:, g5.slot, :], mixed[4][:], x_mid[2][:, g5.slot, :], ALU.add).then_inc(x_ready[4], 1)
                if g2:
                    dve.wait_ge(exp_done[1], g2.count())
                    dve.reciprocal(rc[0][:], sm[0][:]).then_inc(recip_done[1], 1)
                if g2:
                    dve.wait_ge(recip_done[1], g2.count())
                    dve.tensor_scalar(sc[0][:, 0, :], sc[0][:, 0, :], rc[0][:], None, ALU.mult).then_inc(norm_done[1], 1)
                if g3:
                    dve.wait_ge(resid_ready[2], g3.count())
                    if g3.has_past(2):
                        dve.wait_ge(x_ready[4], g3.count(back=2))
                    dve.scalar_tensor_tensor(out=x_mid[2][:, g3.slot, :], in0=mixed[2][:], scalar=0.0, in1=tmp[1][:, 0, :],
                                             op0=ALU.max, op1=ALU.add).then_inc(x_ready[2], 1)
                if g2:
                    dve.wait_ge(att_hi_ready[1], g2.count())
                    dve.tensor_tensor(att_lo[0][:].rearrange("p h n -> p (h n)"), serial[0][:, 0:P], att_hi[0][:].rearrange("p h n -> p (h n)").bitcast(F32),
                                      ALU.subtract).then_inc(att_lo_ready[1], 1)
                if g3:
                    dve.wait_ge(x_ready[2], g3.count())
                    dve.bn_stats(st[3][:], x_mid[2][:, g3.slot, :]).then_inc(stats_done[3], 1)
                if g3:
                    dve.wait_ge(stats_done[3], g3.count())
                    dve.sem_inc(wait_passed, 1)
                    dve.bn_aggr(mv[3][:], st[3][:]).then_inc(moments_ready[3], 1)

            for k in range(4):
                dve.memset(rows_r[k][:].bitcast(F32), 0.0).then_inc(rows_cleared, 1)
            dve.wait_ge(rows_cleared, 4)
            in_turns(dve, B, turn)


def kernel(x, adj, L0_gnn_W, L0_gnn_a, L1_gnn_W, L1_gnn_a, L2_gnn_W_fc, L2_gnn_W_attn, L3_gnn_W1,
           L3_gnn_att_src1, L3_gnn_att_dst1, L3_gnn_b1, L3_gnn_W2, L3_gnn_att_src2, L3_gnn_att_dst2,
           L3_gnn_b2):
    import numpy as np
    import concourse.bacc as bacc
    from concourse.bass_utils import run_bass_kernel_spmd

    heads = L3_gnn_att_src1.shape[0]
    sel = np.zeros((KSEL, 2 + 2 * heads, P), np.float32)
    for part in (0, LOROW):
        for vec in range(2):
            for hl in range(2):
                sel[part + 2 * hl + vec, vec] = 1.0
                for h in range(heads):
                    sel[part + 2 * heads * hl + heads * vec + h, 2 + heads * vec + h] = 1.0
    named = dict(x=x, adj=adj, w0=L0_gnn_W, a0=L0_gnn_a, w1=L1_gnn_W, a1=L1_gnn_a, wfc=L2_gnn_W_fc,
                 afc=L2_gnn_W_attn, w3=L3_gnn_W1, as3=L3_gnn_att_src1, ad3=L3_gnn_att_dst1, b3=L3_gnn_b1,
                 w4=L3_gnn_W2, as4=L3_gnn_att_src2, ad4=L3_gnn_att_dst2, b4=L3_gnn_b2,
                 ident=np.eye(P, dtype=np.float32), sel=sel)
    nc = bacc.Bacc("TRN2", target_bir_lowering=False, num_devices=1)
    arrays, args = {}, {}
    for name, a in named.items():
        arrays[f"in_{name}"] = np.ascontiguousarray(a)
        args[name] = nc.dram_tensor(f"in_{name}", a.shape, mybir.dt.from_np(arrays[f"in_{name}"].dtype),
                                    kind="ExternalInput").ap()
    out = nc.dram_tensor("out", x.shape, F32, kind="ExternalOutput").ap()
    gat_layers_kernel(nc, out=out, **args)
    return run_bass_kernel_spmd(nc, [arrays], core_ids=[0]).results[0]["out"]
```
